# Optimizing a Trainium2 kernel written in Bass

```python
import numpy as np
import jax
import jax.numpy as jnp

def _softmax(x, axis=-1):
    return jax.nn.softmax(x, axis=axis)

def _gelu(x):
    return jax.nn.gelu(x, approximate=True)

def _silu(x):
    return jax.nn.silu(x)

def _sigmoid(x):
    return jax.nn.sigmoid(x)

def _layernorm(x, axis=-1, eps=1e-05):
    m = jnp.mean(x, axis=axis, keepdims=True)
    v = jnp.var(x, axis=axis, keepdims=True)
    return (x - m) / jnp.sqrt(v + eps)

def _scatter_add(tgt, idx, src, axis=0):
    return tgt.at[idx].add(src)

def _segment_sum(src, seg, n):
    return jax.ops.segment_sum(src, seg, n)
kernel_name = 'mk_seq_postln_d1_jaxref_r8_340118'

def setup_inputs(seed: int=0):
    np.random.seed(seed)
    _w = jnp.asarray

    def _L0_attn_setup():
        import jax, jax.numpy as jnp
        import numpy as np
        import math
        N_EMBD = 128
        N_HEAD = 16
        HEAD = N_EMBD // N_HEAD
        LAMBDA_INIT = 0.8 - 0.6 * math.exp(-0.3 * (4 - 1))
        EPS = 1e-05
        key = jax.random.key(seed)
        ks = jax.random.split(key, 12)
        s = 1.0 / math.sqrt(N_EMBD)
        inp = {'x': jax.random.normal(ks[0], (2, 256, N_EMBD), dtype=jnp.float32), 'q1_w': jax.random.normal(ks[1], (N_EMBD, N_EMBD), dtype=jnp.float32) * s, 'q2_w': jax.random.normal(ks[2], (N_EMBD, N_EMBD), dtype=jnp.float32) * s, 'k1_w': jax.random.normal(ks[3], (N_EMBD, N_EMBD), dtype=jnp.float32) * s, 'k2_w': jax.random.normal(ks[4], (N_EMBD, N_EMBD), dtype=jnp.float32) * s, 'v_w': jax.random.normal(ks[5], (N_EMBD, 2 * N_EMBD), dtype=jnp.float32) * s, 'c_w': jax.random.normal(ks[6], (2 * N_EMBD, N_EMBD), dtype=jnp.float32) * (1.0 / math.sqrt(2 * N_EMBD)), 'lambda_q1': jax.random.normal(ks[7], (N_HEAD, HEAD), dtype=jnp.float32) * 0.1, 'lambda_k1': jax.random.normal(ks[8], (N_HEAD, HEAD), dtype=jnp.float32) * 0.1, 'lambda_q2': jax.random.normal(ks[9], (N_HEAD, HEAD), dtype=jnp.float32) * 0.1, 'lambda_k2': jax.random.normal(ks[10], (N_HEAD, HEAD), dtype=jnp.float32) * 0.1}
        return inp
    _L0_attn_in = _L0_attn_setup()

    def _L0_ffn_setup():
        import jax, jax.numpy as jnp
        import numpy as np
        B, S, DIM = (4, 256, 128)
        E, K, HID = (8, 2, 512)
        key = jax.random.key(seed)
        ks = jax.random.split(key, 8)
        init = lambda k, sh: jax.random.normal(k, sh, jnp.float32) * 0.02
        return {'x': jax.random.normal(ks[0], (B, S, DIM), jnp.float32), 'gate_w': init(ks[1], (DIM, E)), 'gate_b': jnp.zeros((E,), jnp.float32), 'w1': init(ks[2], (E, DIM, HID)), 'b1': jnp.zeros((E, HID), jnp.float32), 'w2': init(ks[3], (E, HID, DIM)), 'b2': jnp.zeros((E, DIM), jnp.float32), 'ws1': init(ks[4], (DIM, HID)), 'bs1': jnp.zeros((HID,), jnp.float32), 'ws2': init(ks[5], (HID, DIM)), 'bs2': jnp.zeros((DIM,), jnp.float32)}
    _L0_ffn_in = _L0_ffn_setup()
    _d = {'L0_attn_x': _L0_attn_in['x'], 'L0_attn_q1_w': _L0_attn_in['q1_w'], 'L0_attn_q2_w': _L0_attn_in['q2_w'], 'L0_attn_k1_w': _L0_attn_in['k1_w'], 'L0_attn_k2_w': _L0_attn_in['k2_w'], 'L0_attn_v_w': _L0_attn_in['v_w'], 'L0_attn_c_w': _L0_attn_in['c_w'], 'L0_attn_lambda_q1': _L0_attn_in['lambda_q1'], 'L0_attn_lambda_k1': _L0_attn_in['lambda_k1'], 'L0_attn_lambda_q2': _L0_attn_in['lambda_q2'], 'L0_attn_lambda_k2': _L0_attn_in['lambda_k2'], 'L0_ffn_gate_w': _L0_ffn_in['gate_w'], 'L0_ffn_gate_b': _L0_ffn_in['gate_b'], 'L0_ffn_w1': _L0_ffn_in['w1'], 'L0_ffn_b1': _L0_ffn_in['b1'], 'L0_ffn_w2': _L0_ffn_in['w2'], 'L0_ffn_b2': _L0_ffn_in['b2'], 'L0_ffn_ws1': _L0_ffn_in['ws1'], 'L0_ffn_bs1': _L0_ffn_in['bs1'], 'L0_ffn_ws2': _L0_ffn_in['ws2'], 'L0_ffn_bs2': _L0_ffn_in['bs2']}
    _x0 = _d['L0_attn_x']
    _d['L0_attn_x'] = jax.random.normal(jax.random.fold_in(jax.random.key(seed), 1), (32, 256, 128), dtype=_x0.dtype)
    del _x0
    return _d

def reference(L0_attn_x, L0_attn_q1_w, L0_attn_q2_w, L0_attn_k1_w, L0_attn_k2_w, L0_attn_v_w, L0_attn_c_w, L0_attn_lambda_q1, L0_attn_lambda_k1, L0_attn_lambda_q2, L0_attn_lambda_k2, L0_ffn_gate_w, L0_ffn_gate_b, L0_ffn_w1, L0_ffn_b1, L0_ffn_w2, L0_ffn_b2, L0_ffn_ws1, L0_ffn_bs1, L0_ffn_ws2, L0_ffn_bs2):

    def _L0_attn_ref(x, q1_w, q2_w, k1_w, k2_w, v_w, c_w, lambda_q1, lambda_k1, lambda_q2, lambda_k2):
        import jax, jax.numpy as jnp
        import numpy as np
        import math
        N_EMBD = 128
        N_HEAD = 16
        HEAD = N_EMBD // N_HEAD
        LAMBDA_INIT = 0.8 - 0.6 * math.exp(-0.3 * (4 - 1))
        EPS = 1e-05
        B, T, C = x.shape
        H, hs = (N_HEAD, HEAD)

        def heads(w, d):
            return (x @ w).reshape(B, T, H, d).transpose(0, 2, 1, 3)
        q1 = heads(q1_w, hs)
        q2 = heads(q2_w, hs)
        k1 = heads(k1_w, hs)
        k2 = heads(k2_w, hs)
        v = heads(v_w, 2 * hs)
        scale = 1.0 / math.sqrt(hs)
        causal = jnp.tril(jnp.ones((T, T), dtype=bool))
        neg = jnp.float32(-jnp.inf)
        att1 = jnp.einsum('bhqd,bhkd->bhqk', q1, k1) * scale
        att2 = jnp.einsum('bhqd,bhkd->bhqk', q2, k2) * scale
        att1 = jax.nn.softmax(jnp.where(causal, att1, neg), axis=-1)
        att2 = jax.nn.softmax(jnp.where(causal, att2, neg), axis=-1)
        lam1 = jnp.exp(jnp.sum(lambda_q1 * lambda_k1, axis=-1))
        lam2 = jnp.exp(jnp.sum(lambda_q2 * lambda_k2, axis=-1))
        lam = (lam1 - lam2 + LAMBDA_INIT)[None, :, None, None]
        att = att1 - lam * att2
        y = jnp.einsum('bhqk,bhkd->bhqd', att, v)
        mu = jnp.mean(y, axis=-1, keepdims=True)
        var = jnp.mean(jnp.square(y - mu), axis=-1, keepdims=True)
        y = (y - mu) / jnp.sqrt(var + EPS)
        y = y * (1.0 - LAMBDA_INIT)
        y = y.transpose(0, 2, 1, 3).reshape(B, T, 2 * C)
        return y @ c_w

    def _L0_ffn_ref(x, gate_w, gate_b, w1, b1, w2, b2, ws1, bs1, ws2, bs2):
        import jax, jax.numpy as jnp
        import numpy as np
        B, S, DIM = (4, 256, 128)
        E, K, HID = (8, 2, 512)
        orig_shape = x.shape
        xf = x.reshape(-1, DIM)
        logits = xf @ gate_w + gate_b
        top_w, top_i = jax.lax.top_k(logits, K)
        gw = jax.nn.softmax(top_w, axis=-1).astype(xf.dtype)
        combine = (gw[:, :, None] * jax.nn.one_hot(top_i, E, dtype=xf.dtype)).sum(axis=1)
        out = jnp.zeros_like(xf)
        for e in range(E):
            h = jax.nn.gelu(xf @ w1[e] + b1[e], approximate=False)
            out = out + combine[:, e:e + 1] * (h @ w2[e] + b2[e])
        shared = jax.nn.gelu(xf @ ws1 + bs1, approximate=False) @ ws2 + bs2
        return (out + shared).reshape(orig_shape)
    x = L0_attn_x
    x = _layernorm(x + _L0_attn_ref(x, L0_attn_q1_w, L0_attn_q2_w, L0_attn_k1_w, L0_attn_k2_w, L0_attn_v_w, L0_attn_c_w, L0_attn_lambda_q1, L0_attn_lambda_k1, L0_attn_lambda_q2, L0_attn_lambda_k2), axis=-1)
    x = _layernorm(x + _L0_ffn_ref(x, L0_ffn_gate_w, L0_ffn_gate_b, L0_ffn_w1, L0_ffn_b1, L0_ffn_w2, L0_ffn_b2, L0_ffn_ws1, L0_ffn_bs1, L0_ffn_ws2, L0_ffn_bs2), axis=-1)
    return x

_drawn_inputs = setup_inputs


def setup_inputs(seed=0):
    import zlib

    import numpy as np

    out = dict(_drawn_inputs(seed))
    spreads = {'L0_ffn_gate_b': (0.0, 0.1),
     'L0_ffn_b1': (0.0, 0.488),
     'L0_ffn_b2': (0.0, 0.1),
     'L0_ffn_bs1': (0.0, 0.373),
     'L0_ffn_bs2': (0.0, 0.1)}
    factors = {'L0_attn_lambda_q1': 3.913,
     'L0_attn_lambda_k1': 4.859,
     'L0_attn_lambda_q2': 4.544,
     'L0_attn_lambda_k2': 3.679}
    for name, (base, spread) in spreads.items():
        noise = np.random.default_rng([zlib.crc32(name.encode()), seed]).standard_normal(out[name].shape)
        drawn = base * np.exp(spread * noise) if base else spread * noise
        out[name] = jnp.asarray(drawn.astype(out[name].dtype))
    for name, factor in factors.items():
        out[name] = (out[name] * factor).astype(out[name].dtype)
    return out
```

```python
import math
from contextlib import ExitStack

import concourse.bass as bass
import concourse.mybir as mybir

B, T, C = 32, 256, 128
H, HS = 16, 8
DV = 2 * HS
P = 128
NQT = T // P
QUADS = H // 4
OCT = QUADS // 2
UNITS = 4
ITEMS = 3 * UNITS
E, HID = 8, 512
HC = HID // P
GT = 512
NG = B * T // GT
TT = GT // P
LAMBDA_INIT = 0.8 - 0.6 * math.exp(-0.3 * (4 - 1))
KEEP = 1.0 - LAMBDA_INIT
EPS = 1e-5
SCALE = 1.0 / math.sqrt(HS)
NEG = -1e30

F32 = mybir.dt.float32
F32R = mybir.dt.float32r
BF16 = mybir.dt.bfloat16
ALU = mybir.AluOpType
ACT = mybir.ActivationFunctionType
AX = mybir.AxisListType


def build(nc, x, q1_w, q2_w, k1_w, k2_w, v_w, c_w, lambda_q1, lambda_k1, lambda_q2, lambda_k2,
          gate_w, gate_b, w1, b1, w2, b2, ws1, bs1, ws2, bs2, out):
    ctx = ExitStack()
    with ctx:
        def sb(name, shape, dt=F32):
            return ctx.enter_context(nc.sbuf_tensor(name, shape, dt))

        def sem(name):
            return ctx.enter_context(nc.semaphore(name))

        x1_dram = nc.dram_tensor("x1_dram", [B, P, NQT, C], F32, kind="Internal").ap()
        t = dict(x=x, q1_w=q1_w, q2_w=q2_w, k1_w=k1_w, k2_w=k2_w, v_w=v_w, c_w=c_w,
                 lambdas=(lambda_q1, lambda_k1, lambda_q2, lambda_k2), x1=x1_dram, out=out)
        banks = [ctx.enter_context(nc.psum_tensor(f"bank{i}", [P, 512], F32)) for i in range(8)]
        ident = sb("ident", [P, P])
        with ExitStack() as own:
            attention(nc, lambda n, s, d=F32: own.enter_context(nc.sbuf_tensor(n, s, d)), sem, banks, ident, t)
        t |= dict(gate_w=gate_w, gate_b=gate_b, w1=w1, b1=b1, w2=w2, b2=b2, ws1=ws1, bs1=bs1, ws2=ws2,
                  bs2=bs2)
        feed_forward(nc, sb, sem, banks, ident, t)


def attention(nc, sb, sem, banks, ident, t):
    ident_bf = sb("ident_bf", [P, P], BF16)
    causal = sb("causal", [P, P], BF16)
    w_raw = sb("w_raw", [P, 4, C])
    w_stack = sb("w_stack", [P, 4, QUADS, 4, 32])
    vw = sb("vw", [P, H * DV])
    cw = sb("cw", [P, 2, C])
    lam_in = sb("lam_in", [P, 4, H * HS])
    lam_prod = sb("lam_prod", [P, 2, H * HS])
    lam_sum = sb("lam_sum", [P, 2, H])
    neg_lam = sb("neg_lam", [P, H])
    pat_row = sb("pat_row", [1, 5, P])
    one = sb("one", [1, 1])
    pat = sb("pat", [P, 5])
    x_in = sb("x_in", [P, NQT, C])
    x_res = sb("x_res", [P, NQT, C])
    xT = sb("xT", [P, T])
    rounded = sb("rounded", [P, 4, 2 * T], F32R)
    q_stack = [sb(f"q_stack{i}", [P, 2, 2, T], F32R) for i in range(2)]
    k_stack = [sb(f"k_stack{i}", [P, 2, 2, T], F32R) for i in range(2)]
    q_diag = [sb(f"q_diag{i}", [P, 2, UNITS, 2 * T], F32R) for i in range(2)]
    k_diag = [sb(f"k_diag{i}", [P, 2, UNITS, 2 * T], F32R) for i in range(2)]
    maxima = sb("maxima", [P, NQT, 2, 2, P])
    v_aug = sb("v_aug", [P, NQT, H, 32])
    probs = [sb(f"probs{i}", [P, ITEMS, 512]) for i in range(2)]
    y_sb = sb("y_sb", [P, 2, 2, T])
    y_rden = sb("y_rden", [P, QUADS, 2, NQT, 4])
    y_norm = sb("y_norm", [P, 2, NQT, H, DV])
    y_diff = sb("y_diff", [P, NQT * H, DV])
    y_cent = sb("y_cent", [P, NQT * H, DV])
    y_sq = sb("y_sq", [P, NQT * H, DV])
    y_sum = sb("y_sum", [P, NQT * H])
    y_mean = sb("y_mean", [P, NQT * H])
    y_var = sb("y_var", [P, NQT * H])
    y_rstd = sb("y_rstd", [P, NQT * H])
    y_out = sb("y_out", [P, NQT, H * DV])
    yT = sb("yT", [P, NQT, 2, P])
    z = sb("z", [P, NQT, C])
    z_stats = sb("z_stats", [P, NQT, 6])
    z_mv = sb("z_mv", [P, NQT, 2])
    z_veps = sb("z_veps", [P, NQT])
    z_rstd = sb("z_rstd", [P, NQT])
    neg_half = sb("neg_half", [P, NQT * H])
    x1 = sb("x1", [P, NQT, C])

    max_bank, exp_bank, y_bank = banks[0:2], banks[2:4], banks[4]
    q_bank, k_bank, t_bank = banks[5], banks[6], banks[7]

    weights_in = sem("weights_in")
    lam_loaded = sem("lam_loaded")
    setup_pool = sem("setup_pool")
    setup_dve = sem("setup_dve")
    lam_exp = sem("lam_exp")
    pat_ready = sem("pat_ready")
    consts_ready = sem("consts_ready")
    x_in_loaded = sem("x_in_loaded")
    x_res_loaded = sem("x_res_loaded")
    xT_ready = sem("xT_ready")
    xT_saved = sem("xT_saved")
    proj_ready = sem("proj_ready")
    round_done = sem("round_done")
    stack_done = sem("stack_done")
    diag_zeroed = sem("diag_zeroed")
    k_diag_in = sem("k_diag_in")
    q_diag_in = sem("q_diag_in")
    v_ready = sem("v_ready")
    v_saved = sem("v_saved")
    max_ready = sem("max_ready")
    max_done = sem("max_done")
    shift_ready = sem("shift_ready")
    shift_done = sem("shift_done")
    exp_ready = sem("exp_ready")
    exp_done = sem("exp_done")
    masked = sem("masked")
    y_ready = sem("y_ready")
    y_saved = sem("y_saved")
    yt_ready = sem("yt_ready")
    y_scaled = sem("y_scaled")
    dve_step = sem("dve_step")
    waits_passed = sem("waits_passed")
    pool_step = sem("pool_step")
    z_counted = sem("z_counted")
    sum_done = sem("sum_done")
    diff_done = sem("diff_done")
    sq_done = sem("sq_done")
    var_done = sem("var_done")
    heads_done = sem("heads_done")
    nT_ready = sem("nT_ready")
    nT_saved = sem("nT_saved")
    cw_ready = sem("cw_ready")
    z_done = sem("z_done")
    mv_done = sem("mv_done")
    veps_done = sem("veps_done")
    rstd_done = sem("rstd_done")
    x1_done = sem("x1_done")
    x1_stored = sem("x1_stored")

    tiled = lambda a: a.rearrange("b (t p) c -> b p t c", p=P)
    x_t = tiled(t["x"])
    LAM_SUM = 4

    def wait_apart(eng, s, value):
        eng.wait_ge(s, value)
        eng.sem_inc(waits_passed, 1)

    def wait(eng, s, value):
        if not isinstance(value, int) or value > 0:
            eng.wait_ge(s, value)

    def loop(eng, iteration):
        iteration(0, True, False)
        with eng.Fori(1, B - 1) as n:
            iteration(n, True, True)
        iteration(B - 1, True, True)
        iteration(B, False, True)

    blk = nc.Block()
    with blk as block:

        @block.sync
        def _(sp):
            sp.sem_inc(x1_stored, 16)
            sp.sem_inc(z_done, 1)
            for i, name in enumerate(("q1_w", "q2_w", "k1_w", "k2_w")):
                sp.dma_start(w_raw[:, i, :], t[name]).then_inc(weights_in, 16)
            sp.dma_start(vw[:], t["v_w"]).then_inc(weights_in, 16)
            sp.dma_start(cw[:], t["c_w"].rearrange("(k p) n -> p k n", p=P)).then_inc(weights_in, 16)
            for i, lam in enumerate(t["lambdas"]):
                row = lam.rearrange("(o h) d -> o (h d)", o=1)
                sp.dma_start(lam_in[:, i, :], row.broadcast_to([P, H * HS])).then_inc(lam_loaded, 16)
            sp.dma_start(x_in[:], x_t[0]).then_inc(x_in_loaded, 16)

            def spread(stacks, diags, arrived, g, quad):
                for u in range(UNITS):
                    r = slice(32 * u, 32 * u + 32)
                    sp.dma_start(diags[g][r, quad, u, :].bitcast(F32),
                                 stacks[g][r, quad].rearrange("p m t -> p (m t)").bitcast(F32)
                                 ).then_inc(arrived, 16)

            def store_x1(n):
                sp.wait_ge(x1_done, n - 1)
                sp.dma_start(t["x1"][n - 2], x1[:]).then_inc(x1_stored, 16)

            sp.wait_ge(diag_zeroed, 4)
            for q in range(2):
                sp.wait_ge(stack_done, 2 * q + 2)
                spread(k_stack, k_diag, k_diag_in, 0, q)

            def iteration(n, start, end):
                if end and not (isinstance(n, int) and n < 2):
                    store_x1(n)
                if start and (not isinstance(n, int) or n < B - 1):
                    sp.wait_ge(xT_ready, n + 1)
                    sp.dma_start(x_in[:], x_t[n + 1]).then_inc(x_in_loaded, 16)
                if end:
                    sp.wait_ge(z_done, n)
                    sp.dma_start(x_res[:], x_t[n - 1]).then_inc(x_res_loaded, 16)
                for g in range(OCT):
                    o = OCT * n + g
                    more = start and (g == 0 or not isinstance(n, int) or n < B - 1)
                    for q in range(2):
                        if more:
                            sp.wait_ge(stack_done, 4 * (o + 1) + 2 * q + 2)
                            spread(k_stack, k_diag, k_diag_in, 1 - g, q)
                        if start:
                            sp.wait_ge(shift_done, 2 * o + q + 1)
                            spread(q_stack, q_diag, q_diag_in, g, q)

            iteration(0, True, False)
            iteration(1, True, True)
            with sp.Fori(2, B - 1) as n:
                iteration(n, True, True)
            iteration(B - 1, True, True)
            iteration(B, False, True)
            store_x1(B + 1)
            sp.wait_ge(x1_stored, 16 * (B + 1))

        @block.gpsimd
        def _(pool):
            nc.gpsimd.memset(ident[:], 0.0).then_inc(setup_pool, 1)
            nc.gpsimd.memset(causal[:], 0.0).then_inc(setup_pool, 1)
            nc.gpsimd.memset(neg_half[:], -0.5).then_inc(setup_pool, 1)
            pool.wait_ge(setup_pool, 3)
            nc.gpsimd.affine_select(out=ident[:], in_=ident[:], compare_op=ALU.not_equal, fill=1.0,
                                    base=0, pattern=[[-1, P]], channel_multiplier=1).then_inc(setup_pool, 1)
            nc.gpsimd.affine_select(out=causal[:], in_=causal[:], compare_op=ALU.is_ge, fill=NEG,
                                    base=0, pattern=[[-1, P]], channel_multiplier=1).then_inc(setup_pool, 1)
            for d in (*q_diag, *k_diag):
                nc.gpsimd.memset(d[:].bitcast(F32), 0.0).then_inc(diag_zeroed, 1)
            pool.wait_ge(setup_pool, 5)
            nc.gpsimd.tensor_copy(ident_bf[:], ident[:]).then_inc(consts_ready, 1)

            def iteration(n, start, end):
                for g in range(OCT):
                    o = OCT * n + g
                    if (g == 0 and end) or (g == 1 and start):
                        pr = probs[1 - g]
                        for j in range(ITEMS):
                            wait_apart(pool, exp_done, ITEMS * (o - 1) + j + 1)
                            if j % 3 == 2:
                                v = pr[:, j, :].rearrange("p (a q) -> p a q", q=P)
                            else:
                                v = pr[:, j, :].rearrange("p (a q) -> p a q", q=T)[:, :, 0:P]
                            nc.gpsimd.affine_select(out=v, in_=v, compare_op=ALU.is_ge, fill=0.0, base=0,
                                                    pattern=[[0, v.shape[1]], [1, P]],
                                                    channel_multiplier=-1).then_inc(masked, 1)
                    if g == 0 and end:
                        bc = lambda a: a[:].unsqueeze(2).broadcast_to([P, NQT * H, DV])
                        half = lambda i: y_norm[:, i].rearrange("p t h d -> p (t h) d")
                        pool.wait_ge(y_scaled, 4 * n)
                        nc.gpsimd.tensor_add(y_diff[:], half(0), half(1)).then_inc(diff_done, 1)
                        wait_apart(pool, sum_done, n)
                        nc.gpsimd.tensor_scalar(y_mean[:], y_sum[:], 1.0 / DV, None,
                                                ALU.mult).then_inc(pool_step, 1)
                        pool.wait_ge(pool_step, 4 * (n - 1) + 1)
                        nc.gpsimd.tensor_sub(y_cent[:], y_diff[:], bc(y_mean)).then_inc(pool_step, 1)
                        pool.wait_ge(pool_step, 4 * (n - 1) + 2)
                        nc.gpsimd.tensor_mul(y_sq[:], y_cent[:], y_cent[:]).then_inc(sq_done, 1)
                        wait_apart(pool, var_done, n)
                        nc.gpsimd.tensor_scalar(y_rstd[:], y_var[:], 1.0 / (DV * KEEP * KEEP), EPS / (KEEP * KEEP),
                                                ALU.mult, ALU.add).then_inc(pool_step, 1)
                        pool.wait_ge(pool_step, 4 * (n - 1) + 3)
                        nc.gpsimd.tensor_tensor(y_mean[:], y_rstd[:], neg_half[:], ALU.pow).then_inc(pool_step, 1)
                        pool.wait_ge(pool_step, 4 * (n - 1) + 4)
                        nc.gpsimd.tensor_mul(y_out[:].rearrange("p t (h d) -> p (t h) d", d=DV), y_cent[:],
                                             bc(y_mean)).then_inc(heads_done, 1)
                    if g == 1 and end:
                        wait_apart(pool, mv_done, n)
                        nc.gpsimd.tensor_scalar(z_veps[:], z_mv[:, :, 1], EPS, None, ALU.add).then_inc(veps_done, 1)
                        pool.wait_ge(veps_done, n)
                        nc.gpsimd.tensor_tensor(z_rstd[:], z_veps[:], neg_half[:, 0:NQT],
                                                ALU.pow).then_inc(rstd_done, 1)

            loop(pool, iteration)

        @block.scalar
        def _(act):
            act.wait_ge(setup_dve, LAM_SUM)
            nc.scalar.activation(lam_sum[:], lam_sum[:], ACT.Exp).then_inc(lam_exp, 1)
            act.wait_ge(pat_ready, 2)

            def save_xT(n):
                act.wait_ge(xT_ready, n + 1)
                nc.scalar.activation(xT[:], k_bank[:, 0:T], ACT.Copy).then_inc(xT_saved, 1)

            def round_proj(o, j):
                act.wait_ge(proj_ready, 4 * o + j + 1)
                if j % 2 == 0:
                    nc.scalar.activation(rounded[:, j, :], q_bank[:], ACT.Copy,
                                         scale=pat[:, 1:2]).then_inc(round_done, 1)
                else:
                    nc.scalar.activation(rounded[:, j, :], k_bank[:], ACT.Identity, scale=pat[:, 3:4],
                                         bias=pat[:, 4:5]).then_inc(round_done, 1)

            def save_y(o, q):
                act.wait_ge(y_ready, 2 * o + q + 1)
                nc.scalar.activation(y_sb[:, q].rearrange("p m t -> p (m t)"), y_bank[:],
                                     ACT.Copy).then_inc(y_saved, 1)

            save_xT(0)
            for j in range(4):
                round_proj(0, j)

            def iteration(n, start, end):
                for g in range(OCT):
                    o = OCT * n + g
                    cur, old = start, (end if g == 0 else start)
                    more = start and (g == 0 or not isinstance(n, int) or n < B - 1)
                    if old:
                        for j in range(ITEMS):
                            act.wait_ge(exp_ready, ITEMS * (o - 1) + j + 1)
                            nc.scalar.activation(probs[1 - g][:, j, :], exp_bank[j % 2][:], ACT.Exp,
                                                 scale=SCALE).then_inc(exp_done, 1)
                    if g == 1 and end:
                        act.wait_ge(nT_ready, n)
                        nc.scalar.activation(yT[:].rearrange("p t k q -> p (t k q)"), t_bank[:],
                                             ACT.Copy).then_inc(nT_saved, 1)
                    if g == 1 and more:
                        save_xT(n + 1)
                    if more:
                        round_proj(o + 1, 0)
                        round_proj(o + 1, 1)
                    if old:
                        save_y(o - 1, 0)
                    if more:
                        round_proj(o + 1, 2)
                        round_proj(o + 1, 3)
                    if old:
                        save_y(o - 1, 1)

            loop(act, iteration)

        @block.vector
        def _(dve):
            chain = [0]

            def link(ins):
                chain[0] += 1
                ins.then_inc(setup_dve, 1)
                dve.wait_ge(setup_dve, chain[0])

            dve.wait_ge(lam_loaded, 64)
            for i in range(2):
                link(nc.vector.tensor_mul(lam_prod[:, i, :], lam_in[:, 2 * i, :], lam_in[:, 2 * i + 1, :]))
                link(nc.vector.reduce_sum(lam_sum[:, i, :],
                                          lam_prod[:, i, :].rearrange("p (h d) -> p h d", d=HS), AX.X))
            rows = pat_row[:].rearrange("o k (r c) -> o k r c", c=32)
            link(nc.vector.memset(pat_row[:], 0.0))
            link(nc.vector.memset(rows[:, 0, :, HS:2 * HS], 1.0))
            link(nc.vector.memset(pat_row[:, 1, :], 1.0))
            link(nc.vector.memset(rows[:, 1, :, HS:2 * HS], -1.0))
            link(nc.vector.memset(rows[:, 2, :, 2 * HS:3 * HS], 1.0))
            link(nc.vector.memset(pat_row[:, 3, :], 1.0))
            link(nc.vector.memset(rows[:, 3, :, 2 * HS:3 * HS], -1.0))
            link(nc.vector.memset(rows[:, 4, :, 3 * HS:3 * HS + 1], -1.0))
            nc.vector.memset(one[:], 1.0).then_inc(pat_ready, 1)
            link(nc.vector.memset(w_stack[:], 0.0))
            dve.wait_ge(weights_in, 96)
            for i in range(4):
                for r in range(3):
                    last = nc.vector.tensor_copy(
                        w_stack[:, i].rearrange("p a b c -> p (a b) c")[:, :, r * HS:(r + 1) * HS],
                        w_raw[:, i, :].rearrange("p (h d) -> p h d", d=HS))
            last.then_inc(consts_ready, 1)
            nc.vector.memset(maxima[:], 0.0)
            link(nc.vector.memset(v_aug[:], 0.0))
            link(nc.vector.memset(v_aug[:, :, :, DV:DV + 1], 1.0))
            dve.wait_ge(lam_exp, 1)
            link(nc.vector.tensor_sub(neg_lam[:], lam_sum[:, 1, :], lam_sum[:, 0, :]))
            link(nc.vector.tensor_scalar_add(neg_lam[:], neg_lam[:], -LAMBDA_INIT))
            dve.wait_ge(consts_ready, 3)
            link(nc.vector.tensor_copy(pat[:], t_bank[:, 0:5]))
            nc.vector.memset(one[:], 1.0).then_inc(pat_ready, 1)

            def stack(o, g, j):
                q = j // 2
                src, keep = (q_bank, pat[:, 0:1]) if j % 2 == 0 else (k_bank, pat[:, 2:3])
                dst = (q_stack if j % 2 == 0 else k_stack)[g]
                dve.wait_ge(round_done, 4 * o + j + 1)
                nc.vector.scalar_tensor_tensor(
                    out=dst[:, q].rearrange("p m t -> p (m t)"), in0=src[:], scalar=keep,
                    in1=rounded[:, j, :], op0=ALU.mult, op1=ALU.add).then_inc(stack_done, 1)

            def save_v(n):
                dve.wait_ge(v_ready, n + 1)
                nc.vector.tensor_copy(v_aug[:, :, :, 0:DV],
                                      k_bank[:].rearrange("p (t h d) -> p t h d", t=NQT, d=DV)
                                      ).then_inc(v_saved, 1)

            def add_shift(o, g, q):
                dve.wait_ge(shift_ready, 2 * o + q + 1)
                dst = q_stack[g][:, q].rearrange("p m t -> p (m t)")
                nc.vector.tensor_add(dst, t_bank[:], dst).then_inc(shift_done, 1)

            def scale_y(o, g, q):
                quad = 2 * g + q
                dve.wait_ge(yt_ready, 2 * o + q + 1)
                v = t_bank[:].rearrange("p (m t h c) -> p m t h c", m=2, t=NQT, c=32)
                nc.vector.reciprocal(y_rden[:, quad], v[:, :, :, :, DV]).then_inc(dve_step, 1)
                dve.wait_ge(dve_step, 4 * o + 2 * q + 1)
                for i in range(NQT):
                    last = nc.vector.tensor_mul(y_rden[:, quad, 1, i], y_rden[:, quad, 1, i],
                                                neg_lam[:, 4 * quad:4 * quad + 4])
                last.then_inc(dve_step, 1)
                dve.wait_ge(dve_step, 4 * o + 2 * q + 2)
                for m in range(2):
                    last = nc.vector.tensor_mul(
                        y_norm[:, m, :, 4 * quad:4 * quad + 4, :], v[:, m, :, :, 0:DV],
                        y_rden[:, quad, m].unsqueeze(3).broadcast_to([P, NQT, 4, DV]))
                last.then_inc(y_scaled, 1)

            for j in range(4):
                stack(0, 0, j)

            def iteration(n, start, end):
                for g in range(OCT):
                    o = OCT * n + g
                    cur, old = start, (end if g == 0 else start)
                    more = start and (g == 0 or not isinstance(n, int) or n < B - 1)
                    if cur:
                        for j in range(ITEMS):
                            row = 32 * (j // 3) + 3 * HS
                            dve.wait_ge(max_ready, ITEMS * o + j + 1)
                            src = max_bank[j % 2][:]
                            if j % 3 == 2:
                                dst = maxima[:, 0, :, :, row]
                                src = src.rearrange("p (a m k) -> p a m k", a=2, k=P)
                            else:
                                dst = maxima[:, 1, j % 3, :, row]
                                src = src.rearrange("p (m k) -> p m k", k=T)
                            nc.vector.reduce_max(dst, src, AX.X).then_inc(max_done, 1)
                    if more:
                        stack(o + 1, 1 - g, 0)
                        stack(o + 1, 1 - g, 1)
                    if cur:
                        add_shift(o, g, 0)
                    if more:
                        stack(o + 1, 1 - g, 2)
                        stack(o + 1, 1 - g, 3)
                    if g == 1 and end:
                        dve.wait_ge(cw_ready, n)
                        dve.wait_ge(x_res_loaded, 16 * n)
                        nc.vector.tensor_add(z[:], t_bank[:, 0:NQT * C].rearrange("p (t c) -> p t c", t=NQT),
                                             x_res[:]).then_inc(z_done, 1)
                    if cur:
                        add_shift(o, g, 1)
                    if old:
                        scale_y(o - 1, 1 - g, 0)
                        scale_y(o - 1, 1 - g, 1)
                    if g == 0 and start:
                        save_v(n)
                    if g == 0 and end:
                        dve.wait_ge(diff_done, n)
                        nc.vector.reduce_sum(y_sum[:], y_diff[:], AX.X).then_inc(sum_done, 1)
                        dve.wait_ge(sq_done, n)
                        nc.vector.reduce_sum(y_var[:], y_sq[:], AX.X).then_inc(var_done, 1)
                    if g == 1 and end:
                        dve.wait_ge(z_done, n + 1)
                        for i in range(NQT):
                            last = nc.vector.bn_stats(z_stats[:, i, :], z[:, i, :])
                        last.then_inc(z_counted, 1)
                        wait_apart(dve, z_counted, n)
                        for i in range(NQT):
                            last = nc.vector.bn_aggr(z_mv[:, i, :], z_stats[:, i, :])
                        last.then_inc(mv_done, 1)
                        dve.wait_ge(rstd_done, n)
                        dve.wait_ge(x1_stored, 16 * n)
                        for i in range(NQT):
                            last = nc.vector.tensor_scalar(x1[:, i, :], z[:, i, :], z_mv[:, i, 0:1],
                                                           z_rstd[:, i:i + 1], ALU.subtract, ALU.mult)
                        last.then_inc(x1_done, 1)

            loop(dve, iteration)

        @block.tensor
        def _(pe):
            mm = nc.tensor.matmul
            pe.wait_ge(pat_ready, 1)
            for i in range(5):
                last = mm(t_bank[:, i:i + 1], pat_row[0:1, i, :], one[0:1, 0:1], start=True, stop=True)
            last.then_inc(consts_ready, 1)
            pe.wait_ge(consts_ready, 3)

            def transpose_x(n):
                pe.wait_ge(x_in_loaded, 16 * (n + 1))
                wait(pe, v_saved, n)
                for i in range(NQT):
                    last = nc.tensor.transpose(k_bank[:, i * P:(i + 1) * P], x_in[:, i, :], ident[:])
                last.then_inc(xT_ready, 1)

            def project(o, g, j):
                quad = 2 * g + j // 2
                bank, m0 = (q_bank, 0) if j % 2 == 0 else (k_bank, 2)
                wait(pe, stack_done, 4 * o + j - 1)
                for m in range(2):
                    last = mm(bank[:, m * T:(m + 1) * T], w_stack[:, m0 + m, quad].rearrange("p a c -> p (a c)"),
                              xT[:], start=(m == 0), stop=(m == 1), skip_group_check=True)
                last.then_inc(proj_ready, 1)

            def values(n):
                pe.wait_ge(stack_done, 4 * (OCT * n + 2))
                for i in range(NQT):
                    last = mm(k_bank[:, i * T:(i + 1) * T], xT[:, i * P:(i + 1) * P], vw[:],
                              start=(i == 0), stop=(i == 1), skip_group_check=True)
                last.then_inc(v_ready, 1)

            def max_scores(o, g, j):
                u, kind = j // 3, j % 3
                bank = max_bank[j % 2]
                if j == 0:
                    pe.wait_ge(stack_done, 4 * (o + 1))
                    pe.wait_ge(k_diag_in, 16 * 2 * UNITS * (o + 1))
                wait(pe, max_done, ITEMS * o + j - 1)
                parts = [(kind, m, 1, T) for m in range(2)] if kind < 2 else \
                        [(a, m, 0, P) for a in range(2) for m in range(2)]
                at = 0
                for k, (a, m, qt, w) in enumerate(parts):
                    mm(bank[:, at:at + w], q_stack[g][:, a, m, qt * P:(qt + 1) * P],
                       k_diag[g][:, a, u, m * T:m * T + w],
                       start=(k == 0), stop=False, skip_group_check=True)
                    at += w
                if kind < 2:
                    dst = bank[:].rearrange("p (m k) -> p m k", k=T)[:, :, P:T]
                else:
                    dst = bank[:].rearrange("p (m k) -> p m k", k=P)
                mask = causal[:].unsqueeze(1).broadcast_to([P, dst.shape[1], P])
                mm(dst, ident_bf[:], mask, start=False, stop=True, skip_group_check=True).then_inc(max_ready, 1)

            def exp_scores(o, g, j):
                u, kind = j // 3, j % 3
                bank = exp_bank[j % 2]
                if j == 0:
                    pe.wait_ge(q_diag_in, 16 * 2 * UNITS * (o + 1))
                wait(pe, exp_done, ITEMS * o + j - 1)
                parts = [(kind, m, 0, 0, T) for m in range(2)] if kind < 2 else \
                        [(a, m, 1, P, P) for a in range(2) for m in range(2)]
                at = 0
                for k, (a, m, kt, q0, w) in enumerate(parts):
                    last = mm(bank[:, at:at + w], k_stack[g][:, a, m, kt * P:(kt + 1) * P],
                              q_diag[g][:, a, u, m * T + q0:m * T + q0 + w], start=(k == 0), stop=(k == len(parts) - 1),
                              skip_group_check=True)
                    at += w
                last.then_inc(exp_ready, 1)

            def shift(o, q):
                if q == 0:
                    pe.wait_ge(max_done, ITEMS * (o + 1))
                    wait(pe, y_scaled, 2 * (o - 1))
                else:
                    pe.wait_ge(shift_done, 2 * o + 1)
                for m in range(2):
                    for i in range(NQT):
                        last = nc.tensor.transpose(t_bank[:, (2 * m + i) * P:(2 * m + i + 1) * P],
                                                   maxima[:, i, q, m, :], ident[:])
                last.then_inc(shift_ready, 1)

            def attend(o, g, q):
                pr = probs[g]
                if q == 0:
                    pe.wait_ge(masked, ITEMS * (o + 1))
                wait(pe, y_saved, 2 * o + q)
                quad = 2 * g + q
                for m in range(2):
                    for kt in range(NQT):
                        for u in range(UNITS):
                            if kt == 0:
                                rhs, q0, w = pr[:, 3 * u + q, m * T:(m + 1) * T], 0, T
                            else:
                                c = (2 * q + m) * P
                                rhs, q0, w = pr[:, 3 * u + 2, c:c + P], P, P
                            last = mm(y_bank[32 * u:32 * u + 32, m * T + q0:m * T + q0 + w],
                                      v_aug[:, kt, 4 * quad + u, :], rhs, start=(kt == 0), stop=(kt == 1))
                last.then_inc(y_ready, 1)

            def transpose_y(o, q):
                if q == 0:
                    wait(pe, y_scaled, 2 * o)
                pe.wait_ge(y_saved, 2 * o + q + 1)
                for m in range(2):
                    for i in range(NQT):
                        last = nc.tensor.transpose(t_bank[:, (2 * m + i) * P:(2 * m + i + 1) * P],
                                                   y_sb[:, q, m, i * P:(i + 1) * P], ident[:])
                last.then_inc(yt_ready, 1)

            transpose_x(0)
            pe.wait_ge(xT_saved, 1)
            for j in range(4):
                project(0, 0, j)

            def iteration(n, start, end):
                for g in range(OCT):
                    o = OCT * n + g
                    cur, old = start, (end if g == 0 else start)
                    more = start and (g == 0 or not isinstance(n, int) or n < B - 1)
                    for j in range(ITEMS):
                        if cur:
                            max_scores(o, g, j)
                        if old:
                            exp_scores(o - 1, 1 - g, j)
                    if g == 1 and end:
                        pe.wait_ge(heads_done, n)
                        pe.wait_ge(y_scaled, 2 * (o - 1))
                        for i in range(NQT):
                            for k in range(2):
                                last = nc.tensor.transpose(t_bank[:, (2 * i + k) * P:(2 * i + k + 1) * P],
                                                           y_out[:, i, k * P:(k + 1) * P], ident[:])
                        last.then_inc(nT_ready, 1)
                    if g == 1 and more:
                        transpose_x(n + 1)
                        pe.wait_ge(xT_saved, n + 2)
                    if more:
                        project(o + 1, 1 - g, 0)
                        project(o + 1, 1 - g, 1)
                    if old:
                        attend(o - 1, 1 - g, 0)
                    if cur:
                        if g == 1 and end:
                            pe.wait_ge(nT_saved, n)
                        shift(o, 0)
                    if more:
                        project(o + 1, 1 - g, 2)
                        project(o + 1, 1 - g, 3)
                    if old:
                        attend(o - 1, 1 - g, 1)
                    if g == 1 and end:
                        if cur:
                            pe.wait_ge(shift_done, 2 * o + 1)
                        pe.wait_ge(nT_saved, n)
                        for i in range(NQT):
                            for k in range(2):
                                last = mm(t_bank[:, i * C:(i + 1) * C], yT[:, i, k, :], cw[:, k, :],
                                          start=(k == 0), stop=(k == 1))
                        last.then_inc(cw_ready, 1)
                        pe.wait_ge(z_done, n + 1)
                    if cur:
                        shift(o, 1)
                        pe.wait_ge(shift_done, 2 * o + 2)
                    if old:
                        transpose_y(o - 1, 0)
                        pe.wait_ge(y_scaled, 2 * (o - 1) + 1)
                        transpose_y(o - 1, 1)
                    if g == 0 and start:
                        values(n)

            loop(pe, iteration)


def feed_forward(nc, sb, sem, banks, ident, t):
    NE = E + 1
    NT = B * T // P
    CH = NE * HC
    gate_w = sb("gate_w", [P, E])
    gate_b = sb("gate_b", [P, E])
    w1_raw = sb("w1_raw", [P, HID])
    w1_hi = sb("w1_hi", [P, NE, HID], F32R)
    w1_lo = sb("w1_lo", [P, NE, HID], F32R)
    w2_sb = sb("w2_sb", [P, NE, HC, C])
    b1_sb = sb("b1_sb", [P, NE, HC])
    b1_rows = sb("b1_rows", [CH, P])
    b2_raw = sb("b2_raw", [1, NE, C])
    b2_hi = sb("b2_hi", [1, NE, C], F32R)
    b2_two = sb("b2_two", [64, NE, C], F32R)
    ones2 = sb("ones2", [64, P], F32R)
    zeros2 = sb("zeros2", [64, NE * C])
    xg = [sb(f"xg{i}", [P, TT, C]) for i in range(2)]
    xt = [sb(f"xt{i}", [P, GT]) for i in range(2)]
    x_hi = sb("x_hi", [P, B * T], F32R)
    x_lo = sb("x_lo", [P, B * T], F32R)
    logits = sb("logits", [P, NT, E])
    rest = sb("rest", [P, NT, E])
    hit = sb("hit", [P, NT, E])
    first = sb("first", [P, NT, E])
    second = sb("second", [P, NT, E])
    comb = sb("comb", [P, NT, E])
    rev = sb("rev", [P, E])
    top1 = sb("top1", [P, NT])
    top2 = sb("top2", [P, NT])
    rank = sb("rank", [P, NT])
    e21 = sb("e21", [P, NT])
    wt1 = sb("wt1", [P, NT])
    wt2 = sb("wt2", [P, NT])
    h = [sb(f"h{i}", [P, GT]) for i in range(2)]
    comb_g = sb("comb_g", [P, TT, E])
    acc = sb("acc", [P, TT, C])
    stats = sb("stats", [P, TT, 6])
    mv = sb("mv", [P, TT, 2])
    veps = sb("veps", [P, TT])
    rstd = sb("rstd", [P, TT])
    minus_half = sb("minus_half", [P, TT])
    out_sb = sb("out_sb", [P, TT, C])

    gate_loaded = sem("gate_loaded")
    w1_loaded = sem("w1_loaded")
    b1_turned = sem("b1_turned")
    w1_split = sem("w1_split")
    w2_loaded = sem("w2_loaded")
    b2_rows = sem("b2_rows")
    b2_ready = sem("b2_ready")
    xg_loaded = [sem(f"xg_loaded{i}") for i in range(2)]
    xt_ready = sem("xt_ready")
    xt_saved = sem("xt_saved")
    xt_split = sem("xt_split")
    logits_ready = sem("logits_ready")
    logits_saved = sem("logits_saved")
    xh_done = sem("xh_done")
    w1_step = sem("w1_step")
    comb_copied = sem("comb_copied")
    gate_step = sem("gate_step")
    gap_done = sem("gap_done")
    gap_exp = sem("gap_exp")
    ffn_consts = sem("ffn_consts")
    xr_loaded = sem("xr_loaded")
    up_ready = sem("up_ready")
    gelu_done = sem("gelu_done")
    down_ready = sem("down_ready")
    combined = sem("combined")
    acc_step = sem("acc_step")
    group_mv = sem("group_mv")
    group_veps = sem("group_veps")
    group_rstd = sem("group_rstd")
    out_done = sem("out_done")
    out_stored = sem("out_stored")
    waits_passed = sem("ffn_waits_passed")

    x1_v = t["x1"]
    PG = GT // T

    def wait(eng, s, value):
        if not isinstance(value, int) or value > 0:
            eng.wait_ge(s, value)

    def load_group(eng, dst, g):
        return eng.dma_start(dst.rearrange("p (b t) c -> p b t c", b=PG),
                             x1_v[bass.ds(g * PG, PG)].rearrange("b p t c -> p b t c"))

    with nc.Block() as block:

        @block.sync
        def _(sp):
            sp.dma_start(gate_w[:], t["gate_w"]).then_inc(gate_loaded, 16)
            sp.dma_start(gate_b[:], t["gate_b"].rearrange("(o e) -> o e", o=1).broadcast_to([P, E])
                         ).then_inc(gate_loaded, 16)
            sp.dma_start(b1_rows[0:HC, :], t["bs1"].rearrange("(k p) -> k p", p=P)).then_inc(gate_loaded, 16)
            sp.dma_start(b1_rows[HC:CH, :], t["b1"].rearrange("e (k p) -> (e k) p", p=P)
                         ).then_inc(gate_loaded, 16)

            def pair(i):
                for p in range(2):
                    wait(sp, xt_ready, 2 * i + p - 1)
                    load_group(sp, xg[p][:], 2 * i + p).then_inc(xg_loaded[p], 16)

            pair(0)
            with sp.Fori(1, NG // 2) as i:
                pair(i)

        @block.tensor
        def _(pe):
            pe.wait_ge(gate_loaded, 64)
            nc.tensor.transpose(banks[4][:, 0:CH], b1_rows[:], ident[0:CH, 0:CH]).then_inc(b1_turned, 1)

            def pair(i):
                for p in range(2):
                    g = 2 * i + p
                    pe.wait_ge(xg_loaded[p], 16 * (i + 1))
                    wait(pe, xt_saved, g - 1)
                    for k in range(TT):
                        last = nc.tensor.transpose(banks[p][:, k * P:(k + 1) * P], xg[p][:, k, :], ident[:])
                    last.then_inc(xt_ready, 1)
                    pe.wait_ge(xt_saved, g + 1)
                    wait(pe, logits_saved, g - 1)
                    for k in range(TT):
                        last = nc.tensor.matmul(banks[2 + p][:, k * E:(k + 1) * E], xt[p][:, k * P:(k + 1) * P],
                                                gate_w[:], start=True, stop=True)
                    last.then_inc(logits_ready, 1)

            pair(0)
            with pe.Fori(1, NG // 2) as i:
                pair(i)

        @block.scalar
        def _(act):
            def pair(i):
                for p in range(2):
                    g = 2 * i + p
                    act.wait_ge(xt_ready, g + 1)
                    wait(act, xt_split, g - 1)
                    nc.scalar.activation(xt[p][:], banks[p][:], ACT.Copy).then_inc(xt_saved, 1)

            pair(0)
            with act.Fori(1, NG // 2) as i:
                pair(i)
            act.wait_ge(gap_done, 1)
            nc.scalar.activation(e21[:], e21[:], ACT.Exp).then_inc(gap_exp, 1)

        @block.vector
        def _(dve):
            dve.wait_ge(gate_loaded, 64)
            dve.wait_ge(b1_turned, 1)
            nc.vector.tensor_copy(b1_sb[:].rearrange("p e k -> p (e k)"), banks[4][:, 0:CH])
            for k in range(E):
                nc.vector.memset(rev[:, k:k + 1], float(E - k))

            def pair(i):
                for p in range(2):
                    g = 2 * i + p
                    dve.wait_ge(xt_saved, g + 1)
                    cols = bass.ds(g * GT, GT)
                    nc.vector.tensor_copy(x_hi[:, cols], xt[p][:]).then_inc(xh_done, 1)
                    dve.wait_ge(xh_done, g + 1)
                    nc.vector.tensor_sub(x_lo[:, cols], xt[p][:], x_hi[:, cols]).then_inc(xt_split, 1)
                    dve.wait_ge(logits_ready, g + 1)
                    nc.vector.tensor_add(logits[:, bass.ds(g * TT, TT), :],
                                         banks[2 + p][:, 0:TT * E].rearrange("p (t e) -> p t e", e=E),
                                         gate_b[:].unsqueeze(1).broadcast_to([P, TT, E])).then_inc(logits_saved, 1)

            pair(0)
            with dve.Fori(1, NG // 2) as i:
                pair(i)
            dve.wait_ge(logits_saved, NG)
            chain = [0]

            def link(ins):
                chain[0] += 1
                ins.then_inc(gate_step, 1)
                dve.wait_ge(gate_step, chain[0])

            per = lambda a: a[:].unsqueeze(2).broadcast_to([P, NT, E])
            rv = rev[:].unsqueeze(1).broadcast_to([P, NT, E])

            def largest(src, top, chosen):
                link(nc.vector.reduce_max(top[:], src[:], AX.X))
                link(nc.vector.tensor_tensor(hit[:], src[:], per(top), ALU.is_equal))
                link(nc.vector.tensor_mul(hit[:], hit[:], rv))
                link(nc.vector.reduce_max(rank[:], hit[:], AX.X))
                link(nc.vector.tensor_tensor(chosen[:], hit[:], per(rank), ALU.is_equal))

            largest(logits, top1, first)
            flat = lambda a: a[:].rearrange("p t e -> p (t e)")
            link(nc.vector.scalar_tensor_tensor(out=flat(rest), in0=flat(first), scalar=NEG, in1=flat(logits),
                                                op0=ALU.mult, op1=ALU.add))
            largest(rest, top2, second)
            nc.vector.tensor_sub(e21[:], top2[:], top1[:]).then_inc(gap_done, 1)
            dve.wait_ge(gap_exp, 1)
            link(nc.vector.tensor_scalar_add(wt2[:], e21[:], 1.0))
            link(nc.vector.reciprocal(wt1[:], wt2[:]))
            link(nc.vector.tensor_mul(wt2[:], e21[:], wt1[:]))
            link(nc.vector.tensor_mul(first[:], first[:], per(wt1)))
            link(nc.vector.tensor_mul(second[:], second[:], per(wt2)))
            link(nc.vector.tensor_add(comb[:], first[:], second[:]))

    with nc.Block() as block:

        @block.sync
        def _(sp):
            sp.dma_start(b2_raw[0:1, 0, :], t["bs2"].rearrange("(o c) -> o c", o=1)).then_inc(w2_loaded, 16)
            sp.dma_start(b2_raw[0:1, 1:NE, :], t["b2"].rearrange("(o e) c -> o e c", o=1)).then_inc(w2_loaded, 16)
            for e in range(NE):
                wait(sp, w1_split, e)
                sp.dma_start(w1_raw[:], t["ws1"] if e == 0 else t["w1"][e - 1]).then_inc(w1_loaded, 16)
            sp.dma_start(w2_sb[:, 0], t["ws2"].rearrange("(k p) c -> p k c", p=P)).then_inc(w2_loaded, 16)
            for e in range(E):
                sp.dma_start(w2_sb[:, e + 1], t["w2"][e].rearrange("(k p) c -> p k c", p=P)
                             ).then_inc(w2_loaded, 16)
            out_v = t["out"].rearrange("b (t p) c -> b p t c", p=P)

            def iteration(g):
                wait(sp, combined, NE * (g - 1) + 1)
                load_group(sp, xg[0][:], g).then_inc(xr_loaded, 16)
                sp.wait_ge(out_done, g + 1)
                sp.dma_start(out_v[bass.ds(g * PG, PG)].rearrange("b p t c -> p b t c"),
                             out_sb[:].rearrange("p (b t) c -> p b t c", b=PG)).then_inc(out_stored, 16)

            iteration(0)
            with sp.Fori(1, NG) as g:
                iteration(g)
            sp.wait_ge(out_stored, 16 * NG)

        @block.gpsimd
        def _(pool):
            nc.gpsimd.memset(minus_half[:], -0.5).then_inc(ffn_consts, 1)
            pool.wait_ge(ffn_consts, 1)

            def iteration(g):
                pool.wait_ge(group_mv, g + 1)
                pool.sem_inc(waits_passed, 1)
                nc.gpsimd.tensor_scalar(veps[:], mv[:, :, 1], EPS, None, ALU.add).then_inc(group_veps, 1)
                pool.wait_ge(group_veps, g + 1)
                nc.gpsimd.tensor_tensor(rstd[:], veps[:], minus_half[:], ALU.pow).then_inc(group_rstd, 1)

            iteration(0)
            with pool.Fori(1, NG) as g:
                iteration(g)

        @block.scalar
        def _(act):
            act.wait_ge(w2_loaded, 16 * (2 + NE))

            def iteration(g):
                for c in range(CH):
                    act.wait_ge(up_ready, CH * g + c + 1)
                    nc.scalar.activation(h[c % 2][:], banks[c % 2][:], ACT.Gelu,
                                         bias=b1_sb[:, c // HC, c % HC:c % HC + 1]).then_inc(gelu_done, 1)

            iteration(0)
            with act.Fori(1, NG) as g:
                iteration(g)

        @block.vector
        def _(dve):
            for e in range(NE):
                dve.wait_ge(w1_loaded, 16 * (e + 1))
                nc.vector.tensor_copy(w1_hi[:, e, :], w1_raw[:]).then_inc(w1_step, 1)
                dve.wait_ge(w1_step, e + 1)
                nc.vector.tensor_sub(w1_lo[:, e, :], w1_raw[:], w1_hi[:, e, :]).then_inc(w1_split, 1)
            nc.vector.memset(zeros2[:], 0.0).then_inc(b2_rows, 1)
            dve.wait_ge(b2_rows, 1)
            dve.wait_ge(w2_loaded, 16 * (2 + NE))
            nc.vector.tensor_copy(b2_two[:].rearrange("r e c -> r (e c)"), zeros2[:])
            nc.vector.tensor_copy(b2_hi[:], b2_raw[:])
            nc.vector.tensor_copy(ones2[:], zeros2[:, 0:P]).then_inc(b2_rows, 1)
            dve.wait_ge(b2_rows, 2)
            nc.vector.tensor_copy(b2_two[0:1], b2_hi[:])
            nc.vector.tensor_sub(b2_two[32:33], b2_raw[:], b2_hi[:])
            for r in (0, 32):
                last = nc.vector.tensor_scalar_add(ones2[r:r + 1, :], zeros2[r:r + 1, 0:P], 1.0)
            last.then_inc(b2_ready, 1)

            def iteration(g):
                nc.vector.tensor_copy(comb_g[:], comb[:, bass.ds(g * TT, TT), :]).then_inc(comb_copied, 1)
                dve.wait_ge(comb_copied, g + 1)
                for e in range(NE):
                    dve.wait_ge(down_ready, NE * g + e + 1)
                    ob = banks[2 + e % 3]
                    if e == 0:
                        dve.wait_ge(xr_loaded, 16 * (g + 1))
                        nc.vector.tensor_add(acc[:], ob[:].rearrange("p (t c) -> p t c", c=C),
                                             xg[0][:]).then_inc(combined, 1)
                    else:
                        dve.wait_ge(combined, NE * g + e)
                        for k in range(TT):
                            last = nc.vector.scalar_tensor_tensor(
                                out=acc[:, k, :], in0=ob[:, k * C:(k + 1) * C],
                                scalar=comb_g[:, k, e - 1:e], in1=acc[:, k, :], op0=ALU.mult, op1=ALU.add)
                        last.then_inc(combined, 1)
                dve.wait_ge(combined, NE * (g + 1))
                for k in range(TT):
                    last = nc.vector.bn_stats(stats[:, k, :], acc[:, k, :])
                last.then_inc(acc_step, 1)
                dve.wait_ge(acc_step, g + 1)
                dve.sem_inc(waits_passed, 1)
                for k in range(TT):
                    last = nc.vector.bn_aggr(mv[:, k, :], stats[:, k, :])
                last.then_inc(group_mv, 1)
                dve.wait_ge(group_rstd, g + 1)
                wait(dve, out_stored, 16 * g)
                for k in range(TT):
                    last = nc.vector.tensor_scalar(out_sb[:, k, :], acc[:, k, :], mv[:, k, 0:1],
                                                   rstd[:, k:k + 1], ALU.subtract, ALU.mult)
                last.then_inc(out_done, 1)

            iteration(0)
            with dve.Fori(1, NG) as g:
                iteration(g)

        @block.tensor
        def _(pe):
            pe.wait_ge(w1_split, NE)
            pe.wait_ge(b2_ready, 1)
            pe.wait_ge(w2_loaded, 16 * (2 + NE))
            mm = nc.tensor.matmul

            def up(g, c):
                e, k = c // HC, c % HC
                cols = bass.ds(g * GT, GT)
                wait(pe, gelu_done, CH * g + c - 1)
                bank = banks[c % 2]
                ks = slice(k * P, (k + 1) * P)
                mm(bank[:], w1_hi[:, e, ks], x_lo[:, cols], start=True, stop=False)
                mm(bank[:], w1_lo[:, e, ks], x_hi[:, cols], start=False, stop=False)
                mm(bank[:], w1_hi[:, e, ks], x_hi[:, cols], start=False, stop=True).then_inc(up_ready, 1)

            def down(g, c):
                e, k = c // HC, c % HC
                ob = banks[2 + e % 3]
                if k == 0:
                    wait(pe, combined, NE * g + e - 2)
                    mm(ob[:], ones2[:], b2_two[:, e, :].unsqueeze(1).broadcast_to([64, TT, C]),
                       start=True, stop=False, skip_group_check=True)
                pe.wait_ge(gelu_done, CH * g + c + 1)
                for j in range(TT):
                    last = mm(ob[:, j * C:(j + 1) * C], h[c % 2][:, j * P:(j + 1) * P], w2_sb[:, e, k, :],
                              start=False, stop=(k == HC - 1), skip_group_check=True)
                if k == HC - 1:
                    last.then_inc(down_ready, 1)

            def iteration(g):
                up(g, 0)
                for c in range(CH):
                    if c + 1 < CH:
                        up(g, c + 1)
                    down(g, c)

            iteration(0)
            with pe.Fori(1, NG) as g:
                iteration(g)


_INS = ["attn_x", "attn_q1_w", "attn_q2_w", "attn_k1_w", "attn_k2_w", "attn_v_w", "attn_c_w",
        "attn_lambda_q1", "attn_lambda_k1", "attn_lambda_q2", "attn_lambda_k2",
        "ffn_gate_w", "ffn_gate_b", "ffn_w1", "ffn_b1", "ffn_w2", "ffn_b2",
        "ffn_ws1", "ffn_bs1", "ffn_ws2", "ffn_bs2"]


def kernel(**inputs):
    import numpy as np
    import concourse.bacc as bacc
    from concourse.bass_utils import run_bass_kernel_spmd

    nc = bacc.Bacc("TRN2", target_bir_lowering=False, num_devices=1)
    arrays, args = {}, []
    for name in _INS:
        a = np.ascontiguousarray(inputs["L0_" + name])
        arrays[f"in_{name}"] = a
        args.append(nc.dram_tensor(f"in_{name}", a.shape, mybir.dt.from_np(a.dtype), kind="ExternalInput").ap())
    args.append(nc.dram_tensor("out", (B, T, C), F32, kind="ExternalOutput").ap())
    build(nc, *args)
    r = run_bass_kernel_spmd(nc, [arrays], core_ids=[0])
    return r.results[0]["out"]
```

```python
import math
from contextlib import ExitStack

import concourse.bass as bass
import concourse.mybir as mybir

B, T, C = 32, 256, 128
H, HS = 16, 8
DV = 2 * HS
P = 128
NQT = T // P
QUADS = H // 4
OCT = QUADS // 2
UNITS = 4
ITEMS = 3 * UNITS
HALF = ITEMS // 2
E, HID = 8, 512
HC = HID // P
GT = 512
NG = B * T // GT
TT = GT // P
LAMBDA_INIT = 0.8 - 0.6 * math.exp(-0.3 * (4 - 1))
KEEP = 1.0 - LAMBDA_INIT
EPS = 1e-5
SCALE = 1.0 / math.sqrt(HS)
NEG = -1e30

F32 = mybir.dt.float32
F32R = mybir.dt.float32r
BF16 = mybir.dt.bfloat16
ALU = mybir.AluOpType
ACT = mybir.ActivationFunctionType
AX = mybir.AxisListType


def build(nc, x, q1_w, q2_w, k1_w, k2_w, v_w, c_w, lambda_q1, lambda_k1, lambda_q2, lambda_k2,
          gate_w, gate_b, w1, b1, w2, b2, ws1, bs1, ws2, bs2, out):
    ctx = ExitStack()
    with ctx:
        def sb(name, shape, dt=F32):
            return ctx.enter_context(nc.sbuf_tensor(name, shape, dt))

        def sem(name):
            return ctx.enter_context(nc.semaphore(name))

        x1_dram = nc.dram_tensor("x1_dram", [B, P, NQT, C], F32, kind="Internal").ap()
        t = dict(x=x, q1_w=q1_w, q2_w=q2_w, k1_w=k1_w, k2_w=k2_w, v_w=v_w, c_w=c_w,
                 lambdas=(lambda_q1, lambda_k1, lambda_q2, lambda_k2), x1=x1_dram, out=out)
        banks = [ctx.enter_context(nc.psum_tensor(f"bank{i}", [P, 512], F32)) for i in range(8)]
        ident = sb("ident", [P, P])
        with ExitStack() as own:
            attention(nc, lambda n, s, d=F32: own.enter_context(nc.sbuf_tensor(n, s, d)), sem, banks, ident, t)
        t |= dict(gate_w=gate_w, gate_b=gate_b, w1=w1, b1=b1, w2=w2, b2=b2, ws1=ws1, bs1=bs1, ws2=ws2,
                  bs2=bs2)
        feed_forward(nc, sb, sem, banks, ident, t)


def attention(nc, sb, sem, banks, ident, t):
    ident_bf = sb("ident_bf", [P, P], BF16)
    causal = sb("causal", [P, P], BF16)
    w_raw = sb("w_raw", [P, 4, C])
    w_stack = sb("w_stack", [P, 4, QUADS, 4, 32])
    w_hi = sb("w_hi", [P, 4, QUADS, 4, 32], F32R)
    w_lo = sb("w_lo", [P, 4, QUADS, 4, 32], F32R)
    vw = sb("vw", [P, H * DV])
    vw_hi = sb("vw_hi", [P, H * DV], F32R)
    vw_lo = sb("vw_lo", [P, H * DV], F32R)
    cw = sb("cw", [P, 2, C])
    lam_in = sb("lam_in", [P, 4, H * HS])
    lam_prod = sb("lam_prod", [P, 2, H * HS])
    lam_sum = sb("lam_sum", [P, 2, H])
    neg_lam = sb("neg_lam", [P, H])
    pat_row = sb("pat_row", [1, 5, P])
    one = sb("one", [1, 1])
    pat = sb("pat", [P, 5])
    x_in = sb("x_in", [P, NQT, C])
    x_res = sb("x_res", [P, NQT, C])
    xT_hi = sb("xT_hi", [P, T], F32R)
    xT_lo = sb("xT_lo", [P, T], F32R)
    rounded = sb("rounded", [P, 4, 2 * T], F32R)
    q_stack = [sb(f"q_stack{i}", [P, 2, 2, T], F32R) for i in range(2)]
    k_stack = [sb(f"k_stack{i}", [P, 2, 2, T], F32R) for i in range(2)]
    q_diag = [sb(f"q_diag{i}", [P, 2, UNITS, 2 * T], F32R) for i in range(2)]
    k_diag = [sb(f"k_diag{i}", [P, 2, UNITS, 2 * T], F32R) for i in range(2)]
    maxima = sb("maxima", [P, NQT, 2, 2, P])
    v_aug = sb("v_aug", [P, NQT, H, 32])
    probs = [sb(f"probs{i}", [P, ITEMS, 512]) for i in range(2)]
    y_sb = sb("y_sb", [P, 2, 2, T])
    y_rden = sb("y_rden", [P, QUADS, 2, NQT, 4])
    y_norm = sb("y_norm", [P, 2, NQT, H, DV])
    y_diff = sb("y_diff", [P, NQT * H, DV])
    y_cent = sb("y_cent", [P, NQT * H, DV])
    y_sq = sb("y_sq", [P, NQT * H, DV])
    y_sum = sb("y_sum", [P, NQT * H])
    y_mean = sb("y_mean", [P, NQT * H])
    y_var = sb("y_var", [P, NQT * H])
    y_rstd = sb("y_rstd", [P, NQT * H])
    y_out = sb("y_out", [P, NQT, H * DV])
    yT = sb("yT", [P, NQT, 2, P])
    z = sb("z", [P, NQT, C])
    z_stats = sb("z_stats", [P, NQT, 6])
    z_mv = sb("z_mv", [P, NQT, 2])
    z_veps = sb("z_veps", [P, NQT])
    z_rstd = sb("z_rstd", [P, NQT])
    neg_half = sb("neg_half", [P, NQT * H])
    x1 = sb("x1", [P, NQT, C])

    max_bank, exp_bank, t_bank = (banks[0], banks[1], banks[4]), banks[2:4], banks[7]
    proj_bank = banks[5:7]
    x_bank = proj_bank[1]
    y_bank = (proj_bank[1], max_bank[2])
    shift_bank = yt_bank = (t_bank, proj_bank[0])

    weights_in = sem("weights_in")
    lam_loaded = sem("lam_loaded")
    setup_pool = sem("setup_pool")
    setup_dve = sem("setup_dve")
    lam_exp = sem("lam_exp")
    pat_ready = sem("pat_ready")
    consts_ready = sem("consts_ready")
    x_in_loaded = sem("x_in_loaded")
    x_res_loaded = sem("x_res_loaded")
    xT_ready = sem("xT_ready")
    xT_hi_done = sem("xT_hi_done")
    xT_saved = sem("xT_saved")
    proj_ready = sem("proj_ready")
    round_done = sem("round_done")
    stack_done = sem("stack_done")
    diag_zeroed = sem("diag_zeroed")
    k_diag_in = [sem(f"k_diag_in{u}") for u in range(UNITS)]
    q_diag_in = [sem(f"q_diag_in{u}") for u in range(UNITS)]
    v_ready = sem("v_ready")
    v_saved = sem("v_saved")
    max_ready = sem("max_ready")
    max_done = sem("max_done")
    shift_ready = sem("shift_ready")
    shift_done = sem("shift_done")
    exp_ready = sem("exp_ready")
    exp_done = sem("exp_done")
    masked = sem("masked")
    y_ready = sem("y_ready")
    y_saved = sem("y_saved")
    yt_ready = sem("yt_ready")
    y_scaled = sem("y_scaled")
    dve_step = sem("dve_step")
    waits_passed = sem("waits_passed")
    pool_step = sem("pool_step")
    z_counted = sem("z_counted")
    sum_done = sem("sum_done")
    diff_done = sem("diff_done")
    sq_done = sem("sq_done")
    var_done = sem("var_done")
    heads_done = sem("heads_done")
    nT_ready = sem("nT_ready")
    nT_saved = sem("nT_saved")
    cw_ready = sem("cw_ready")
    z_done = sem("z_done")
    mv_done = sem("mv_done")
    veps_done = sem("veps_done")
    rstd_done = sem("rstd_done")
    x1_done = sem("x1_done")
    x1_stored = sem("x1_stored")

    tiled = lambda a: a.rearrange("b (t p) c -> b p t c", p=P)
    x_t = tiled(t["x"])
    LAM_SUM = 4

    def wait_apart(eng, s, value):
        eng.wait_ge(s, value)
        eng.sem_inc(waits_passed, 1)

    def wait(eng, s, value):
        if not isinstance(value, int) or value > 0:
            eng.wait_ge(s, value)

    def loop(eng, iteration):
        iteration(0, True, False)
        with eng.Fori(1, B - 1) as n:
            iteration(n, True, True)
        iteration(B - 1, True, True)
        iteration(B, False, True)

    blk = nc.Block()
    with blk as block:

        @block.sync
        def _(sp):
            sp.sem_inc(x1_stored, 16)
            sp.sem_inc(z_done, 1)
            for i, name in enumerate(("q1_w", "q2_w", "k1_w", "k2_w")):
                sp.dma_start(w_raw[:, i, :], t[name]).then_inc(weights_in, 16)
            sp.dma_start(vw[:], t["v_w"]).then_inc(weights_in, 16)
            sp.dma_start(cw[:], t["c_w"].rearrange("(k p) n -> p k n", p=P)).then_inc(weights_in, 16)
            for i, lam in enumerate(t["lambdas"]):
                row = lam.rearrange("(o h) d -> o (h d)", o=1)
                sp.dma_start(lam_in[:, i, :], row.broadcast_to([P, H * HS])).then_inc(lam_loaded, 16)
            sp.dma_start(x_in[:], x_t[0]).then_inc(x_in_loaded, 16)

            def spread(stacks, diags, arrived, g):
                for u in range(UNITS):
                    r = slice(32 * u, 32 * u + 32)
                    sp.dma_start(diags[g][r, :, u, :].bitcast(F32),
                                 stacks[g][r].rearrange("p a m t -> p a (m t)").bitcast(F32)
                                 ).then_inc(arrived[u], 16)

            def store_x1(n):
                sp.wait_ge(x1_done, n - 1)
                sp.dma_start(t["x1"][n - 2], x1[:]).then_inc(x1_stored, 16)

            sp.wait_ge(diag_zeroed, 4)
            sp.wait_ge(stack_done, 2)
            spread(k_stack, k_diag, k_diag_in, 0)

            def iteration(n, start, end):
                if end and not (isinstance(n, int) and n < 2):
                    store_x1(n)
                if start and (not isinstance(n, int) or n < B - 1):
                    sp.wait_ge(xT_ready, n + 1)
                    sp.dma_start(x_in[:], x_t[n + 1]).then_inc(x_in_loaded, 16)
                if end:
                    sp.wait_ge(z_done, n)
                    sp.dma_start(x_res[:], x_t[n - 1]).then_inc(x_res_loaded, 16)
                for g in range(OCT):
                    o = OCT * n + g
                    more = start and (g == 0 or not isinstance(n, int) or n < B - 1)
                    if start:
                        sp.wait_ge(shift_done, 2 * o + 2)
                        spread(q_stack, q_diag, q_diag_in, g)
                    if more:
                        sp.wait_ge(stack_done, 4 * (o + 1) + 2)
                        spread(k_stack, k_diag, k_diag_in, 1 - g)

            iteration(0, True, False)
            iteration(1, True, True)
            with sp.Fori(2, B - 1) as n:
                iteration(n, True, True)
            iteration(B - 1, True, True)
            iteration(B, False, True)
            store_x1(B + 1)
            sp.wait_ge(x1_stored, 16 * (B + 1))

        @block.gpsimd
        def _(pool):
            nc.gpsimd.memset(ident[:], 0.0).then_inc(setup_pool, 1)
            nc.gpsimd.memset(causal[:], 0.0).then_inc(setup_pool, 1)
            nc.gpsimd.memset(neg_half[:], -0.5).then_inc(setup_pool, 1)
            pool.wait_ge(setup_pool, 3)
            nc.gpsimd.affine_select(out=ident[:], in_=ident[:], compare_op=ALU.not_equal, fill=1.0,
                                    base=0, pattern=[[-1, P]], channel_multiplier=1).then_inc(setup_pool, 1)
            nc.gpsimd.affine_select(out=causal[:], in_=causal[:], compare_op=ALU.is_ge, fill=NEG,
                                    base=0, pattern=[[-1, P]], channel_multiplier=1).then_inc(setup_pool, 1)
            for d in (*q_diag, *k_diag):
                nc.gpsimd.memset(d[:].bitcast(F32), 0.0).then_inc(diag_zeroed, 1)
            pool.wait_ge(setup_pool, 5)
            nc.gpsimd.tensor_copy(ident_bf[:], ident[:]).then_inc(consts_ready, 1)

            def mask(o, g, items):
                for j in items:
                    wait_apart(pool, exp_done, ITEMS * o + j + 1)
                    if j % 3 == 2:
                        v = probs[g][:, j, :].rearrange("p (a q) -> p a q", q=P)
                    else:
                        v = probs[g][:, j, :].rearrange("p (a q) -> p a q", q=T)[:, :, 0:P]
                    nc.gpsimd.affine_select(out=v, in_=v, compare_op=ALU.is_ge, fill=0.0, base=0,
                                            pattern=[[0, v.shape[1]], [1, P]],
                                            channel_multiplier=-1).then_inc(masked, 1)

            bc = lambda a: a[:].unsqueeze(2).broadcast_to([P, NQT * H, DV])

            def centre_heads(n):
                wait_apart(pool, sum_done, n)
                nc.gpsimd.tensor_scalar(y_mean[:], y_sum[:], 1.0 / DV, None, ALU.mult).then_inc(pool_step, 1)
                pool.wait_ge(pool_step, 4 * (n - 1) + 1)
                nc.gpsimd.tensor_sub(y_cent[:], y_diff[:], bc(y_mean)).then_inc(pool_step, 1)
                pool.wait_ge(pool_step, 4 * (n - 1) + 2)
                nc.gpsimd.tensor_mul(y_sq[:], y_cent[:], y_cent[:]).then_inc(sq_done, 1)

            def scale_heads(n):
                wait_apart(pool, var_done, n)
                nc.gpsimd.tensor_scalar(y_rstd[:], y_var[:], 1.0 / (DV * KEEP * KEEP), EPS / (KEEP * KEEP),
                                        ALU.mult, ALU.add).then_inc(pool_step, 1)
                pool.wait_ge(pool_step, 4 * (n - 1) + 3)
                nc.gpsimd.tensor_tensor(y_mean[:], y_rstd[:], neg_half[:], ALU.pow).then_inc(pool_step, 1)
                pool.wait_ge(pool_step, 4 * (n - 1) + 4)
                nc.gpsimd.tensor_mul(y_out[:].rearrange("p t (h d) -> p (t h) d", d=DV), y_cent[:],
                                     bc(y_mean)).then_inc(heads_done, 1)

            def residual_rstd(n):
                wait_apart(pool, mv_done, n)
                nc.gpsimd.tensor_scalar(z_veps[:], z_mv[:, :, 1], EPS, None, ALU.add).then_inc(veps_done, 1)
                pool.wait_ge(veps_done, n)
                nc.gpsimd.tensor_tensor(z_rstd[:], z_veps[:], neg_half[:, 0:NQT], ALU.pow).then_inc(rstd_done, 1)

            def iteration(n, start, end):
                for g in range(OCT):
                    o = OCT * n + g
                    cur, old = start, (end if g == 0 else start)
                    if old:
                        mask(o - 1, 1 - g, range(HALF, ITEMS))
                    if g == 1 and end:
                        scale_heads(n)
                    if cur:
                        mask(o, g, range(HALF // 2))
                    if g == 1 and end:
                        residual_rstd(n)
                    if cur:
                        mask(o, g, range(HALF // 2, HALF))
                    if g == 0 and end:
                        centre_heads(n)

            loop(pool, iteration)

        @block.scalar
        def _(act):
            act.wait_ge(setup_dve, LAM_SUM)
            nc.scalar.activation(lam_sum[:], lam_sum[:], ACT.Exp).then_inc(lam_exp, 1)
            act.wait_ge(pat_ready, 2)

            def round_proj(o, j):
                act.wait_ge(proj_ready, 4 * o + j + 1)
                if j < 2:
                    nc.scalar.activation(rounded[:, j, :], proj_bank[j][:], ACT.Identity, scale=pat[:, 3:4],
                                         bias=pat[:, 4:5]).then_inc(round_done, 1)
                else:
                    nc.scalar.activation(rounded[:, j, :], proj_bank[j % 2][:], ACT.Copy,
                                         scale=pat[:, 1:2]).then_inc(round_done, 1)

            def save_y(o, q):
                act.wait_ge(y_ready, 2 * o + q + 1)
                nc.scalar.activation(y_sb[:, q].rearrange("p m t -> p (m t)"), y_bank[q][:],
                                     ACT.Copy).then_inc(y_saved, 1)

            for j in range(4):
                round_proj(0, j)

            def exponentials(o, g, items):
                for j in items:
                    act.wait_ge(exp_ready, ITEMS * o + j + 1)
                    nc.scalar.activation(probs[g][:, j, :], exp_bank[j % 2][:], ACT.Exp,
                                         scale=SCALE).then_inc(exp_done, 1)

            def iteration(n, start, end):
                for g in range(OCT):
                    o = OCT * n + g
                    cur, old = start, (end if g == 0 else start)
                    more = start and (g == 0 or not isinstance(n, int) or n < B - 1)
                    if old:
                        exponentials(o - 1, 1 - g, range(HALF, ITEMS))
                        save_y(o - 1, 0)
                    if more:
                        round_proj(o + 1, 0)
                    if old:
                        save_y(o - 1, 1)
                    if more:
                        round_proj(o + 1, 1)
                        round_proj(o + 1, 2)
                        round_proj(o + 1, 3)
                    if g == 1 and end:
                        act.wait_ge(nT_ready, n)
                        nc.scalar.activation(yT[:].rearrange("p t k q -> p (t k q)"), t_bank[:],
                                             ACT.Copy).then_inc(nT_saved, 1)
                    if cur:
                        exponentials(o, g, range(HALF))

            loop(act, iteration)

        @block.vector
        def _(dve):
            chain = [0]

            def link(ins):
                chain[0] += 1
                ins.then_inc(setup_dve, 1)
                dve.wait_ge(setup_dve, chain[0])

            dve.wait_ge(lam_loaded, 64)
            for i in range(2):
                link(nc.vector.tensor_mul(lam_prod[:, i, :], lam_in[:, 2 * i, :], lam_in[:, 2 * i + 1, :]))
                link(nc.vector.reduce_sum(lam_sum[:, i, :],
                                          lam_prod[:, i, :].rearrange("p (h d) -> p h d", d=HS), AX.X))
            rows = pat_row[:].rearrange("o k (r c) -> o k r c", c=32)
            link(nc.vector.memset(pat_row[:], 0.0))
            link(nc.vector.memset(rows[:, 0, :, HS:2 * HS], 1.0))
            link(nc.vector.memset(pat_row[:, 1, :], 1.0))
            link(nc.vector.memset(rows[:, 1, :, HS:2 * HS], -1.0))
            link(nc.vector.memset(rows[:, 2, :, 2 * HS:3 * HS], 1.0))
            link(nc.vector.memset(pat_row[:, 3, :], 1.0))
            link(nc.vector.memset(rows[:, 3, :, 2 * HS:3 * HS], -1.0))
            link(nc.vector.memset(rows[:, 4, :, 3 * HS:3 * HS + 1], -1.0))
            nc.vector.memset(one[:], 1.0).then_inc(pat_ready, 1)
            link(nc.vector.memset(w_stack[:], 0.0))
            dve.wait_ge(weights_in, 96)
            for i in range(4):
                for r in range(3):
                    last = nc.vector.tensor_copy(
                        w_stack[:, i].rearrange("p a b c -> p (a b) c")[:, :, r * HS:(r + 1) * HS],
                        w_raw[:, i, :].rearrange("p (h d) -> p h d", d=HS))
            link(last)
            link(nc.vector.tensor_copy(w_hi[:], w_stack[:]))
            link(nc.vector.tensor_sub(w_lo[:], w_stack[:], w_hi[:]))
            link(nc.vector.tensor_copy(vw_hi[:], vw[:]))
            nc.vector.tensor_sub(vw_lo[:], vw[:], vw_hi[:]).then_inc(consts_ready, 1)
            nc.vector.memset(maxima[:], 0.0)
            link(nc.vector.memset(v_aug[:], 0.0))
            link(nc.vector.memset(v_aug[:, :, :, DV:DV + 1], 1.0))
            dve.wait_ge(lam_exp, 1)
            link(nc.vector.tensor_sub(neg_lam[:], lam_sum[:, 1, :], lam_sum[:, 0, :]))
            link(nc.vector.tensor_scalar_add(neg_lam[:], neg_lam[:], -LAMBDA_INIT))
            dve.wait_ge(consts_ready, 3)
            link(nc.vector.tensor_copy(pat[:], t_bank[:, 0:5]))
            nc.vector.memset(one[:], 1.0).then_inc(pat_ready, 1)

            def stack(o, g, j):
                q = j % 2
                src, keep = proj_bank[q], (pat[:, 2:3] if j < 2 else pat[:, 0:1])
                dst = (k_stack if j < 2 else q_stack)[g]
                dve.wait_ge(round_done, 4 * o + j + 1)
                nc.vector.scalar_tensor_tensor(
                    out=dst[:, q].rearrange("p m t -> p (m t)"), in0=src[:], scalar=keep,
                    in1=rounded[:, j, :], op0=ALU.mult, op1=ALU.add).then_inc(stack_done, 1)

            def save_v(n):
                dve.wait_ge(v_ready, n + 1)
                nc.vector.tensor_copy(v_aug[:, :, :, 0:DV],
                                      x_bank[:].rearrange("p (t h d) -> p t h d", t=NQT, d=DV)
                                      ).then_inc(v_saved, 1)

            def add_shift(o, g, q):
                dve.wait_ge(shift_ready, 2 * o + q + 1)
                dst = q_stack[g][:, q].rearrange("p m t -> p (m t)")
                nc.vector.tensor_add(dst, shift_bank[q][:], dst).then_inc(shift_done, 1)

            def scale_y(o, g, q):
                quad = 2 * g + q
                dve.wait_ge(yt_ready, 2 * o + q + 1)
                v = yt_bank[q][:].rearrange("p (m t h c) -> p m t h c", m=2, t=NQT, c=32)
                nc.vector.reciprocal(y_rden[:, quad], v[:, :, :, :, DV]).then_inc(dve_step, 1)
                dve.wait_ge(dve_step, 4 * o + 2 * q + 1)
                for i in range(NQT):
                    last = nc.vector.tensor_mul(y_rden[:, quad, 1, i], y_rden[:, quad, 1, i],
                                                neg_lam[:, 4 * quad:4 * quad + 4])
                last.then_inc(dve_step, 1)
                dve.wait_ge(dve_step, 4 * o + 2 * q + 2)
                for m in range(2):
                    last = nc.vector.tensor_mul(
                        y_norm[:, m, :, 4 * quad:4 * quad + 4, :], v[:, m, :, :, 0:DV],
                        y_rden[:, quad, m].unsqueeze(3).broadcast_to([P, NQT, 4, DV]))
                last.then_inc(y_scaled, 1)

            def save_xT(n):
                dve.wait_ge(xT_ready, n + 1)
                nc.vector.tensor_copy(xT_hi[:], x_bank[:, 0:T]).then_inc(xT_hi_done, 1)
                dve.wait_ge(xT_hi_done, n + 1)
                nc.vector.tensor_sub(xT_lo[:], x_bank[:, 0:T], xT_hi[:]).then_inc(xT_saved, 1)

            save_xT(0)
            for j in range(4):
                stack(0, 0, j)

            def maximum(o, g, j):
                row = 32 * (j // 3) + 3 * HS
                dve.wait_ge(max_ready, ITEMS * o + j + 1)
                src = max_bank[j % 3][:]
                if j % 3 == 2:
                    dst = maxima[:, 0, :, :, row]
                    src = src.rearrange("p (a m k) -> p a m k", a=2, k=P)
                else:
                    dst = maxima[:, 1, j % 3, :, row]
                    src = src.rearrange("p (m k) -> p m k", k=T)
                nc.vector.reduce_max(dst, src, AX.X).then_inc(max_done, 1)

            def residual(n):
                dve.wait_ge(cw_ready, n)
                dve.wait_ge(x_res_loaded, 16 * n)
                nc.vector.tensor_add(z[:], t_bank[:, 0:NQT * C].rearrange("p (t c) -> p t c", t=NQT),
                                     x_res[:]).then_inc(z_done, 1)
                dve.wait_ge(z_done, n + 1)
                for i in range(NQT):
                    last = nc.vector.bn_stats(z_stats[:, i, :], z[:, i, :])
                last.then_inc(z_counted, 1)
                wait_apart(dve, z_counted, n)
                for i in range(NQT):
                    last = nc.vector.bn_aggr(z_mv[:, i, :], z_stats[:, i, :])
                last.then_inc(mv_done, 1)

            half = lambda i: y_norm[:, i].rearrange("p t h d -> p (t h) d")

            def sum_heads(n):
                dve.wait_ge(y_scaled, 4 * n)
                nc.vector.tensor_add(y_diff[:], half(0), half(1)).then_inc(diff_done, 1)
                dve.wait_ge(diff_done, n)
                nc.vector.reduce_sum(y_sum[:], y_diff[:], AX.X).then_inc(sum_done, 1)

            def normalize(n):
                dve.wait_ge(rstd_done, n)
                dve.wait_ge(x1_stored, 16 * n)
                for i in range(NQT):
                    last = nc.vector.tensor_scalar(x1[:, i, :], z[:, i, :], z_mv[:, i, 0:1],
                                                   z_rstd[:, i:i + 1], ALU.subtract, ALU.mult)
                last.then_inc(x1_done, 1)

            def iteration(n, start, end):
                for g in range(OCT):
                    o = OCT * n + g
                    cur, old = start, (end if g == 0 else start)
                    more = start and (g == 0 or not isinstance(n, int) or n < B - 1)
                    for j in range(ITEMS):
                        if cur:
                            maximum(o, g, j)
                        if j == 3 and g == 0 and end and not (isinstance(n, int) and n < 2):
                            normalize(n - 1)
                        if j == 3 and g == 1 and end:
                            dve.wait_ge(sq_done, n)
                            nc.vector.reduce_sum(y_var[:], y_sq[:], AX.X).then_inc(var_done, 1)
                        if j == HALF and g == 1 and more:
                            save_xT(n + 1)
                    if cur:
                        add_shift(o, g, 0)
                        add_shift(o, g, 1)
                    if more:
                        for j in range(4):
                            stack(o + 1, 1 - g, j)
                    if g == 1 and end:
                        residual(n)
                    if old:
                        scale_y(o - 1, 1 - g, 0)
                        scale_y(o - 1, 1 - g, 1)
                    if g == 0 and end:
                        sum_heads(n)
                    if g == 0 and start:
                        save_v(n)

            iteration(0, True, False)
            iteration(1, True, True)
            with dve.Fori(2, B - 1) as n:
                iteration(n, True, True)
            iteration(B - 1, True, True)
            iteration(B, False, True)
            normalize(B)

        @block.tensor
        def _(pe):
            mm = nc.tensor.matmul
            pe.wait_ge(pat_ready, 1)
            for i in range(5):
                last = mm(t_bank[:, i:i + 1], pat_row[0:1, i, :], one[0:1, 0:1], start=True, stop=True)
            last.then_inc(consts_ready, 1)
            pe.wait_ge(consts_ready, 3)

            def transpose_x(n):
                pe.wait_ge(x_in_loaded, 16 * (n + 1))
                wait(pe, v_saved, n)
                for i in range(NQT):
                    last = nc.tensor.transpose(x_bank[:, i * P:(i + 1) * P], x_in[:, i, :], ident[:])
                last.then_inc(xT_ready, 1)

            def product3(dst, a_hi, a_lo, b_hi, b_lo, first):
                mm(dst, a_lo, b_hi, start=first, stop=False, skip_group_check=True)
                mm(dst, a_hi, b_lo, start=False, stop=False, skip_group_check=True)
                return mm(dst, a_hi, b_hi, start=False, stop=True, skip_group_check=True)

            def project(o, g, j):
                quad = 2 * g + j % 2
                bank, m0 = proj_bank[j % 2], (2 if j < 2 else 0)
                wait(pe, stack_done, 4 * o + j - 1)
                for m in range(2):
                    hi, lo = (w[:, m0 + m, quad].rearrange("p a c -> p (a c)") for w in (w_hi, w_lo))
                    last = product3(bank[:, m * T:(m + 1) * T], hi, lo, xT_hi[:], xT_lo[:], m == 0)
                last.then_inc(proj_ready, 1)

            def values(n):
                pe.wait_ge(stack_done, 4 * (OCT * n + 2))
                for i in range(NQT):
                    r = slice(i * P, (i + 1) * P)
                    last = product3(x_bank[:, i * T:(i + 1) * T], xT_hi[:, r], xT_lo[:, r], vw_hi[:], vw_lo[:],
                                    i == 0)
                last.then_inc(v_ready, 1)

            def max_scores(o, g, j):
                u, kind = j // 3, j % 3
                bank = max_bank[kind]
                if j == 0:
                    pe.wait_ge(stack_done, 4 * (o + 1))
                if kind == 0:
                    pe.wait_ge(k_diag_in[u], 16 * (o + 1))
                wait(pe, max_done, ITEMS * o + j - 2)
                parts = [(kind, m, 1, T) for m in range(2)] if kind < 2 else \
                        [(a, m, 0, P) for a in range(2) for m in range(2)]
                at = 0
                for k, (a, m, qt, w) in enumerate(parts):
                    mm(bank[:, at:at + w], q_stack[g][:, a, m, qt * P:(qt + 1) * P],
                       k_diag[g][:, a, u, m * T:m * T + w],
                       start=(k == 0), stop=False, skip_group_check=True)
                    at += w
                if kind < 2:
                    dst = bank[:].rearrange("p (m k) -> p m k", k=T)[:, :, P:T]
                else:
                    dst = bank[:].rearrange("p (m k) -> p m k", k=P)
                mask = causal[:].unsqueeze(1).broadcast_to([P, dst.shape[1], P])
                mm(dst, ident_bf[:], mask, start=False, stop=True, skip_group_check=True).then_inc(max_ready, 1)

            def exp_scores(o, g, j):
                u, kind = j // 3, j % 3
                bank = exp_bank[j % 2]
                if kind == 0:
                    pe.wait_ge(q_diag_in[u], 16 * (o + 1))
                wait(pe, exp_done, ITEMS * o + j - 1)
                parts = [(kind, m, 0, 0, T) for m in range(2)] if kind < 2 else \
                        [(a, m, 1, P, P) for a in range(2) for m in range(2)]
                at = 0
                for k, (a, m, kt, q0, w) in enumerate(parts):
                    last = mm(bank[:, at:at + w], k_stack[g][:, a, m, kt * P:(kt + 1) * P],
                              q_diag[g][:, a, u, m * T + q0:m * T + q0 + w], start=(k == 0), stop=(k == len(parts) - 1),
                              skip_group_check=True)
                    at += w
                last.then_inc(exp_ready, 1)

            def shift(o, q):
                if q == 0:
                    pe.wait_ge(max_done, ITEMS * (o + 1))
                    wait(pe, y_scaled, 2 * (o - 1))
                for m in range(2):
                    for i in range(NQT):
                        last = nc.tensor.transpose(shift_bank[q][:, (2 * m + i) * P:(2 * m + i + 1) * P],
                                                   maxima[:, i, q, m, :], ident[:])
                last.then_inc(shift_ready, 1)

            def attend(o, g, q, m):
                if q == 0 and m == 0:
                    pe.wait_ge(masked, ITEMS * (o + 1))
                    wait(pe, y_saved, 2 * o)
                quad = 2 * g + q
                for kt in range(NQT):
                    for u in range(UNITS):
                        if kt == 0:
                            rhs, q0, w = probs[g][:, 3 * u + q, m * T:(m + 1) * T], 0, T
                        else:
                            c = (2 * q + m) * P
                            rhs, q0, w = probs[g][:, 3 * u + 2, c:c + P], P, P
                        last = mm(y_bank[q][32 * u:32 * u + 32, m * T + q0:m * T + q0 + w],
                                  v_aug[:, kt, 4 * quad + u, :], rhs, start=(kt == 0), stop=(kt == 1))
                if m == 1:
                    last.then_inc(y_ready, 1)

            def transpose_y(o, q):
                wait(pe, y_scaled, 2 * o)
                pe.wait_ge(y_saved, 2 * o + q + 1)
                for m in range(2):
                    for i in range(NQT):
                        last = nc.tensor.transpose(yt_bank[q][:, (2 * m + i) * P:(2 * m + i + 1) * P],
                                                   y_sb[:, q, m, i * P:(i + 1) * P], ident[:])
                last.then_inc(yt_ready, 1)

            transpose_x(0)
            pe.wait_ge(xT_saved, 1)
            for j in range(4):
                project(0, 0, j)

            def transpose_heads(n):
                pe.wait_ge(heads_done, n)
                for i in range(NQT):
                    for k in range(2):
                        last = nc.tensor.transpose(t_bank[:, (2 * i + k) * P:(2 * i + k + 1) * P],
                                                   y_out[:, i, k * P:(k + 1) * P], ident[:])
                last.then_inc(nT_ready, 1)

            def project_out(n):
                pe.wait_ge(nT_saved, n)
                for i in range(NQT):
                    for k in range(2):
                        last = mm(t_bank[:, i * C:(i + 1) * C], yT[:, i, k, :], cw[:, k, :],
                                  start=(k == 0), stop=(k == 1))
                last.then_inc(cw_ready, 1)

            late = (0, 1, 3, 4, 6, 7)

            def iteration(n, start, end):
                for g in range(OCT):
                    o = OCT * n + g
                    cur, old = start, (end if g == 0 else start)
                    more = start and (g == 0 or not isinstance(n, int) or n < B - 1)
                    for j in range(ITEMS):
                        if cur:
                            max_scores(o, g, j)
                        if old and j in late:
                            exp_scores(o - 1, 1 - g, HALF + late.index(j))
                        if g == 1 and more and j == HALF:
                            transpose_x(n + 1)
                    if g == 1 and old:
                        pe.wait_ge(v_saved, n + 1)
                    if g == 1 and more:
                        pe.wait_ge(xT_saved, n + 2)
                    if old:
                        attend(o - 1, 1 - g, 0, 0)
                        attend(o - 1, 1 - g, 0, 1)
                    if cur:
                        shift(o, 0)
                        shift(o, 1)
                    if old:
                        attend(o - 1, 1 - g, 1, 0)
                    if cur:
                        pe.wait_ge(shift_done, 2 * o + 2)
                    if more:
                        project(o + 1, 1 - g, 0)
                    if old:
                        attend(o - 1, 1 - g, 1, 1)
                    if more:
                        if old:
                            pe.wait_ge(y_saved, 2 * o - 1)
                        project(o + 1, 1 - g, 1)
                    if g == 0 and old:
                        transpose_y(o - 1, 0)
                    if more:
                        project(o + 1, 1 - g, 2)
                        project(o + 1, 1 - g, 3)
                    if g == 1 and end:
                        transpose_heads(n)
                    for j in range(HALF):
                        if g == 0 and old and j == 2:
                            if more:
                                pe.wait_ge(stack_done, 4 * (o + 1) + 3)
                            transpose_y(o - 1, 1)
                        if g == 0 and start and j == 3:
                            values(n)
                        if g == 1 and end and j == 2:
                            project_out(n)
                        if g == 1 and old and j == 4:
                            if end:
                                pe.wait_ge(z_done, n + 1)
                            transpose_y(o - 1, 0)
                        if g == 1 and old and j == 5:
                            if more:
                                pe.wait_ge(stack_done, 4 * (o + 1) + 3)
                            transpose_y(o - 1, 1)
                        if cur:
                            exp_scores(o, g, j)

            loop(pe, iteration)


def feed_forward(nc, sb, sem, banks, ident, t):
    NE = E + 1
    NT = B * T // P
    CH = NE * HC
    gate_w = sb("gate_w", [P, E])
    gate_b = sb("gate_b", [P, E])
    w1_raw = sb("w1_raw", [P, HID])
    w1_hi = sb("w1_hi", [P, NE, HID], F32R)
    w1_lo = sb("w1_lo", [P, NE, HID], F32R)
    w2_sb = sb("w2_sb", [P, NE, HC, C])
    b1_sb = sb("b1_sb", [P, NE, HC])
    b1_rows = sb("b1_rows", [CH, P])
    b2_raw = sb("b2_raw", [1, NE, C])
    b2_hi = sb("b2_hi", [1, NE, C], F32R)
    b2_two = sb("b2_two", [64, NE, C], F32R)
    ones2 = sb("ones2", [64, P], F32R)
    zeros2 = sb("zeros2", [64, NE * C])
    xg = [sb(f"xg{i}", [P, TT, C]) for i in range(2)]
    xt = [sb(f"xt{i}", [P, GT]) for i in range(2)]
    x_hi = sb("x_hi", [P, B * T], F32R)
    x_lo = sb("x_lo", [P, B * T], F32R)
    logits = sb("logits", [P, NT, E])
    rest = sb("rest", [P, NT, E])
    hit = sb("hit", [P, NT, E])
    first = sb("first", [P, NT, E])
    second = sb("second", [P, NT, E])
    comb = sb("comb", [P, NT, E])
    rev = sb("rev", [P, E])
    top1 = sb("top1", [P, NT])
    top2 = sb("top2", [P, NT])
    rank = sb("rank", [P, NT])
    e21 = sb("e21", [P, NT])
    wt1 = sb("wt1", [P, NT])
    wt2 = sb("wt2", [P, NT])
    h = [sb(f"h{i}", [P, GT]) for i in range(2)]
    comb_g = sb("comb_g", [P, TT, E])
    acc = sb("acc", [P, TT, C])
    stats = sb("stats", [P, TT, 6])
    mv = sb("mv", [P, TT, 2])
    veps = sb("veps", [P, TT])
    rstd = sb("rstd", [P, TT])
    minus_half = sb("minus_half", [P, TT])
    out_sb = sb("out_sb", [P, TT, C])

    gate_loaded = sem("gate_loaded")
    w1_loaded = sem("w1_loaded")
    b1_turned = sem("b1_turned")
    w1_split = sem("w1_split")
    w2_loaded = sem("w2_loaded")
    b2_rows = sem("b2_rows")
    b2_ready = sem("b2_ready")
    xg_loaded = [sem(f"xg_loaded{i}") for i in range(2)]
    xt_ready = sem("xt_ready")
    xt_saved = sem("xt_saved")
    xt_split = sem("xt_split")
    logits_ready = sem("logits_ready")
    logits_saved = sem("logits_saved")
    xh_done = sem("xh_done")
    w1_step = sem("w1_step")
    comb_copied = sem("comb_copied")
    gate_step = sem("gate_step")
    gap_done = sem("gap_done")
    gap_exp = sem("gap_exp")
    ffn_consts = sem("ffn_consts")
    xr_loaded = sem("xr_loaded")
    up_ready = sem("up_ready")
    gelu_done = sem("gelu_done")
    down_ready = sem("down_ready")
    combined = sem("combined")
    acc_step = sem("acc_step")
    group_mv = sem("group_mv")
    group_veps = sem("group_veps")
    group_rstd = sem("group_rstd")
    out_done = sem("out_done")
    out_stored = sem("out_stored")
    waits_passed = sem("ffn_waits_passed")

    x1_v = t["x1"]
    PG = GT // T

    def wait(eng, s, value):
        if not isinstance(value, int) or value > 0:
            eng.wait_ge(s, value)

    def load_group(eng, dst, g):
        return eng.dma_start(dst.rearrange("p (b t) c -> p b t c", b=PG),
                             x1_v[bass.ds(g * PG, PG)].rearrange("b p t c -> p b t c"))

    with nc.Block() as block:

        @block.sync
        def _(sp):
            sp.dma_start(gate_w[:], t["gate_w"]).then_inc(gate_loaded, 16)
            sp.dma_start(gate_b[:], t["gate_b"].rearrange("(o e) -> o e", o=1).broadcast_to([P, E])
                         ).then_inc(gate_loaded, 16)
            sp.dma_start(b1_rows[0:HC, :], t["bs1"].rearrange("(k p) -> k p", p=P)).then_inc(gate_loaded, 16)
            sp.dma_start(b1_rows[HC:CH, :], t["b1"].rearrange("e (k p) -> (e k) p", p=P)
                         ).then_inc(gate_loaded, 16)

            def pair(i):
                for p in range(2):
                    wait(sp, xt_ready, 2 * i + p - 1)
                    load_group(sp, xg[p][:], 2 * i + p).then_inc(xg_loaded[p], 16)

            pair(0)
            with sp.Fori(1, NG // 2) as i:
                pair(i)

        @block.tensor
        def _(pe):
            pe.wait_ge(gate_loaded, 64)
            nc.tensor.transpose(banks[4][:, 0:CH], b1_rows[:], ident[0:CH, 0:CH]).then_inc(b1_turned, 1)

            def pair(i):
                for p in range(2):
                    g = 2 * i + p
                    pe.wait_ge(xg_loaded[p], 16 * (i + 1))
                    wait(pe, xt_saved, g - 1)
                    for k in range(TT):
                        last = nc.tensor.transpose(banks[p][:, k * P:(k + 1) * P], xg[p][:, k, :], ident[:])
                    last.then_inc(xt_ready, 1)
                    pe.wait_ge(xt_saved, g + 1)
                    wait(pe, logits_saved, g - 1)
                    for k in range(TT):
                        last = nc.tensor.matmul(banks[2 + p][:, k * E:(k + 1) * E], xt[p][:, k * P:(k + 1) * P],
                                                gate_w[:], start=True, stop=True)
                    last.then_inc(logits_ready, 1)

            pair(0)
            with pe.Fori(1, NG // 2) as i:
                pair(i)

        @block.scalar
        def _(act):
            def pair(i):
                for p in range(2):
                    g = 2 * i + p
                    act.wait_ge(xt_ready, g + 1)
                    wait(act, xt_split, g - 1)
                    nc.scalar.activation(xt[p][:], banks[p][:], ACT.Copy).then_inc(xt_saved, 1)

            pair(0)
            with act.Fori(1, NG // 2) as i:
                pair(i)
            act.wait_ge(gap_done, 1)
            nc.scalar.activation(e21[:], e21[:], ACT.Exp).then_inc(gap_exp, 1)

        @block.vector
        def _(dve):
            dve.wait_ge(gate_loaded, 64)
            dve.wait_ge(b1_turned, 1)
            nc.vector.tensor_copy(b1_sb[:].rearrange("p e k -> p (e k)"), banks[4][:, 0:CH])
            for k in range(E):
                nc.vector.memset(rev[:, k:k + 1], float(E - k))

            def pair(i):
                for p in range(2):
                    g = 2 * i + p
                    dve.wait_ge(xt_saved, g + 1)
                    cols = bass.ds(g * GT, GT)
                    nc.vector.tensor_copy(x_hi[:, cols], xt[p][:]).then_inc(xh_done, 1)
                    dve.wait_ge(xh_done, g + 1)
                    nc.vector.tensor_sub(x_lo[:, cols], xt[p][:], x_hi[:, cols]).then_inc(xt_split, 1)
                    dve.wait_ge(logits_ready, g + 1)
                    nc.vector.tensor_add(logits[:, bass.ds(g * TT, TT), :],
                                         banks[2 + p][:, 0:TT * E].rearrange("p (t e) -> p t e", e=E),
                                         gate_b[:].unsqueeze(1).broadcast_to([P, TT, E])).then_inc(logits_saved, 1)

            pair(0)
            with dve.Fori(1, NG // 2) as i:
                pair(i)
            dve.wait_ge(logits_saved, NG)
            chain = [0]

            def link(ins):
                chain[0] += 1
                ins.then_inc(gate_step, 1)
                dve.wait_ge(gate_step, chain[0])

            per = lambda a: a[:].unsqueeze(2).broadcast_to([P, NT, E])
            rv = rev[:].unsqueeze(1).broadcast_to([P, NT, E])

            def largest(src, top, chosen):
                link(nc.vector.reduce_max(top[:], src[:], AX.X))
                link(nc.vector.tensor_tensor(hit[:], src[:], per(top), ALU.is_equal))
                link(nc.vector.tensor_mul(hit[:], hit[:], rv))
                link(nc.vector.reduce_max(rank[:], hit[:], AX.X))
                link(nc.vector.tensor_tensor(chosen[:], hit[:], per(rank), ALU.is_equal))

            largest(logits, top1, first)
            flat = lambda a: a[:].rearrange("p t e -> p (t e)")
            link(nc.vector.scalar_tensor_tensor(out=flat(rest), in0=flat(first), scalar=NEG, in1=flat(logits),
                                                op0=ALU.mult, op1=ALU.add))
            largest(rest, top2, second)
            nc.vector.tensor_sub(e21[:], top2[:], top1[:]).then_inc(gap_done, 1)
            dve.wait_ge(gap_exp, 1)
            link(nc.vector.tensor_scalar_add(wt2[:], e21[:], 1.0))
            link(nc.vector.reciprocal(wt1[:], wt2[:]))
            link(nc.vector.tensor_mul(wt2[:], e21[:], wt1[:]))
            link(nc.vector.tensor_mul(first[:], first[:], per(wt1)))
            link(nc.vector.tensor_mul(second[:], second[:], per(wt2)))
            link(nc.vector.tensor_add(comb[:], first[:], second[:]))

    with nc.Block() as block:

        @block.sync
        def _(sp):
            sp.dma_start(b2_raw[0:1, 0, :], t["bs2"].rearrange("(o c) -> o c", o=1)).then_inc(w2_loaded, 16)
            sp.dma_start(b2_raw[0:1, 1:NE, :], t["b2"].rearrange("(o e) c -> o e c", o=1)).then_inc(w2_loaded, 16)
            for e in range(NE):
                wait(sp, w1_split, e)
                sp.dma_start(w1_raw[:], t["ws1"] if e == 0 else t["w1"][e - 1]).then_inc(w1_loaded, 16)
            sp.dma_start(w2_sb[:, 0], t["ws2"].rearrange("(k p) c -> p k c", p=P)).then_inc(w2_loaded, 16)
            for e in range(E):
                sp.dma_start(w2_sb[:, e + 1], t["w2"][e].rearrange("(k p) c -> p k c", p=P)
                             ).then_inc(w2_loaded, 16)
            out_v = t["out"].rearrange("b (t p) c -> b p t c", p=P)

            def iteration(g):
                wait(sp, combined, NE * (g - 1) + 1)
                load_group(sp, xg[0][:], g).then_inc(xr_loaded, 16)
                sp.wait_ge(out_done, g + 1)
                sp.dma_start(out_v[bass.ds(g * PG, PG)].rearrange("b p t c -> p b t c"),
                             out_sb[:].rearrange("p (b t) c -> p b t c", b=PG)).then_inc(out_stored, 16)

            iteration(0)
            with sp.Fori(1, NG) as g:
                iteration(g)
            sp.wait_ge(out_stored, 16 * NG)

        @block.gpsimd
        def _(pool):
            nc.gpsimd.memset(minus_half[:], -0.5).then_inc(ffn_consts, 1)
            pool.wait_ge(ffn_consts, 1)

            def iteration(g):
                pool.wait_ge(group_mv, g + 1)
                pool.sem_inc(waits_passed, 1)
                nc.gpsimd.tensor_scalar(veps[:], mv[:, :, 1], EPS, None, ALU.add).then_inc(group_veps, 1)
                pool.wait_ge(group_veps, g + 1)
                nc.gpsimd.tensor_tensor(rstd[:], veps[:], minus_half[:], ALU.pow).then_inc(group_rstd, 1)

            iteration(0)
            with pool.Fori(1, NG) as g:
                iteration(g)

        @block.scalar
        def _(act):
            act.wait_ge(w2_loaded, 16 * (2 + NE))

            def iteration(g):
                for c in range(CH):
                    act.wait_ge(up_ready, CH * g + c + 1)
                    nc.scalar.activation(h[c % 2][:], banks[c % 2][:], ACT.Gelu,
                                         bias=b1_sb[:, c // HC, c % HC:c % HC + 1]).then_inc(gelu_done, 1)

            iteration(0)
            with act.Fori(1, NG) as g:
                iteration(g)

        @block.vector
        def _(dve):
            for e in range(NE):
                dve.wait_ge(w1_loaded, 16 * (e + 1))
                nc.vector.tensor_copy(w1_hi[:, e, :], w1_raw[:]).then_inc(w1_step, 1)
                dve.wait_ge(w1_step, e + 1)
                nc.vector.tensor_sub(w1_lo[:, e, :], w1_raw[:], w1_hi[:, e, :]).then_inc(w1_split, 1)
            nc.vector.memset(zeros2[:], 0.0).then_inc(b2_rows, 1)
            dve.wait_ge(b2_rows, 1)
            dve.wait_ge(w2_loaded, 16 * (2 + NE))
            nc.vector.tensor_copy(b2_two[:].rearrange("r e c -> r (e c)"), zeros2[:])
            nc.vector.tensor_copy(b2_hi[:], b2_raw[:])
            nc.vector.tensor_copy(ones2[:], zeros2[:, 0:P]).then_inc(b2_rows, 1)
            dve.wait_ge(b2_rows, 2)
            nc.vector.tensor_copy(b2_two[0:1], b2_hi[:])
            nc.vector.tensor_sub(b2_two[32:33], b2_raw[:], b2_hi[:])
            for r in (0, 32):
                last = nc.vector.tensor_scalar_add(ones2[r:r + 1, :], zeros2[r:r + 1, 0:P], 1.0)
            last.then_inc(b2_ready, 1)

            def iteration(g):
                nc.vector.tensor_copy(comb_g[:], comb[:, bass.ds(g * TT, TT), :]).then_inc(comb_copied, 1)
                dve.wait_ge(comb_copied, g + 1)
                for e in range(NE):
                    dve.wait_ge(down_ready, NE * g + e + 1)
                    ob = banks[2 + e % 3]
                    if e == 0:
                        dve.wait_ge(xr_loaded, 16 * (g + 1))
                        nc.vector.tensor_add(acc[:], ob[:].rearrange("p (t c) -> p t c", c=C),
                                             xg[0][:]).then_inc(combined, 1)
                    else:
                        dve.wait_ge(combined, NE * g + e)
                        for k in range(TT):
                            last = nc.vector.scalar_tensor_tensor(
                                out=acc[:, k, :], in0=ob[:, k * C:(k + 1) * C],
                                scalar=comb_g[:, k, e - 1:e], in1=acc[:, k, :], op0=ALU.mult, op1=ALU.add)
                        last.then_inc(combined, 1)
                dve.wait_ge(combined, NE * (g + 1))
                for k in range(TT):
                    last = nc.vector.bn_stats(stats[:, k, :], acc[:, k, :])
                last.then_inc(acc_step, 1)
                dve.wait_ge(acc_step, g + 1)
                dve.sem_inc(waits_passed, 1)
                for k in range(TT):
                    last = nc.vector.bn_aggr(mv[:, k, :], stats[:, k, :])
                last.then_inc(group_mv, 1)
                dve.wait_ge(group_rstd, g + 1)
                wait(dve, out_stored, 16 * g)
                for k in range(TT):
                    last = nc.vector.tensor_scalar(out_sb[:, k, :], acc[:, k, :], mv[:, k, 0:1],
                                                   rstd[:, k:k + 1], ALU.subtract, ALU.mult)
                last.then_inc(out_done, 1)

            iteration(0)
            with dve.Fori(1, NG) as g:
                iteration(g)

        @block.tensor
        def _(pe):
            pe.wait_ge(w1_split, NE)
            pe.wait_ge(b2_ready, 1)
            pe.wait_ge(w2_loaded, 16 * (2 + NE))
            mm = nc.tensor.matmul

            def up(g, c):
                e, k = c // HC, c % HC
                cols = bass.ds(g * GT, GT)
                wait(pe, gelu_done, CH * g + c - 1)
                bank = banks[c % 2]
                ks = slice(k * P, (k + 1) * P)
                mm(bank[:], w1_hi[:, e, ks], x_lo[:, cols], start=True, stop=False)
                mm(bank[:], w1_lo[:, e, ks], x_hi[:, cols], start=False, stop=False)
                mm(bank[:], w1_hi[:, e, ks], x_hi[:, cols], start=False, stop=True).then_inc(up_ready, 1)

            def down(g, c):
                e, k = c // HC, c % HC
                ob = banks[2 + e % 3]
                if k == 0:
                    wait(pe, combined, NE * g + e - 2)
                    mm(ob[:], ones2[:], b2_two[:, e, :].unsqueeze(1).broadcast_to([64, TT, C]),
                       start=True, stop=False, skip_group_check=True)
                pe.wait_ge(gelu_done, CH * g + c + 1)
                for j in range(TT):
                    last = mm(ob[:, j * C:(j + 1) * C], h[c % 2][:, j * P:(j + 1) * P], w2_sb[:, e, k, :],
                              start=False, stop=(k == HC - 1), skip_group_check=True)
                if k == HC - 1:
                    last.then_inc(down_ready, 1)

            def iteration(g):
                up(g, 0)
                for c in range(CH):
                    if c + 1 < CH:
                        up(g, c + 1)
                    down(g, c)

            iteration(0)
            with pe.Fori(1, NG) as g:
                iteration(g)


_INS = ["attn_x", "attn_q1_w", "attn_q2_w", "attn_k1_w", "attn_k2_w", "attn_v_w", "attn_c_w",
        "attn_lambda_q1", "attn_lambda_k1", "attn_lambda_q2", "attn_lambda_k2",
        "ffn_gate_w", "ffn_gate_b", "ffn_w1", "ffn_b1", "ffn_w2", "ffn_b2",
        "ffn_ws1", "ffn_bs1", "ffn_ws2", "ffn_bs2"]


def kernel(**inputs):
    import numpy as np
    import concourse.bacc as bacc
    from concourse.bass_utils import run_bass_kernel_spmd

    nc = bacc.Bacc("TRN2", target_bir_lowering=False, num_devices=1)
    arrays, args = {}, []
    for name in _INS:
        a = np.ascontiguousarray(inputs["L0_" + name])
        arrays[f"in_{name}"] = a
        args.append(nc.dram_tensor(f"in_{name}", a.shape, mybir.dt.from_np(a.dtype), kind="ExternalInput").ap())
    args.append(nc.dram_tensor("out", (B, T, C), F32, kind="ExternalOutput").ap())
    build(nc, *args)
    r = run_bass_kernel_spmd(nc, [arrays], core_ids=[0])
    return r.results[0]["out"]
```

```python
import math
from contextlib import ExitStack

import concourse.bass as bass
import concourse.mybir as mybir

B, T, C = 32, 256, 128
H, HS = 16, 8
DV = 2 * HS
P = 128
NQT = T // P
QUADS = H // 4
OCT = QUADS // 2
UNITS = 4
ITEMS = 3 * UNITS
EARLY = 4
E, HID = 8, 512
HC = HID // P
GT = 512
NG = B * T // GT
TT = GT // P
LAMBDA_INIT = 0.8 - 0.6 * math.exp(-0.3 * (4 - 1))
KEEP = 1.0 - LAMBDA_INIT
EPS = 1e-5
SCALE = 1.0 / math.sqrt(HS)
NEG = -1e30

F32 = mybir.dt.float32
F32R = mybir.dt.float32r
BF16 = mybir.dt.bfloat16
ALU = mybir.AluOpType
ACT = mybir.ActivationFunctionType
AX = mybir.AxisListType


def build(nc, x, q1_w, q2_w, k1_w, k2_w, v_w, c_w, lambda_q1, lambda_k1, lambda_q2, lambda_k2,
          gate_w, gate_b, w1, b1, w2, b2, ws1, bs1, ws2, bs2, out):
    ctx = ExitStack()
    with ctx:
        def sb(name, shape, dt=F32):
            return ctx.enter_context(nc.sbuf_tensor(name, shape, dt))

        def sem(name):
            return ctx.enter_context(nc.semaphore(name))

        x1_dram = nc.dram_tensor("x1_dram", [B, P, NQT, C], F32, kind="Internal").ap()
        t = dict(x=x, q1_w=q1_w, q2_w=q2_w, k1_w=k1_w, k2_w=k2_w, v_w=v_w, c_w=c_w,
                 lambdas=(lambda_q1, lambda_k1, lambda_q2, lambda_k2), x1=x1_dram, out=out)
        banks = [ctx.enter_context(nc.psum_tensor(f"bank{i}", [P, 512], F32)) for i in range(8)]
        ident = sb("ident", [P, P])
        with ExitStack() as own:
            attention(nc, lambda n, s, d=F32: own.enter_context(nc.sbuf_tensor(n, s, d)), sem, banks, ident, t)
        t |= dict(gate_w=gate_w, gate_b=gate_b, w1=w1, b1=b1, w2=w2, b2=b2, ws1=ws1, bs1=bs1, ws2=ws2,
                  bs2=bs2)
        feed_forward(nc, sb, sem, banks, ident, t)


def attention(nc, sb, sem, banks, ident, t):
    ident_bf = sb("ident_bf", [P, P], BF16)
    causal = sb("causal", [P, P], BF16)
    w_raw = sb("w_raw", [P, 4, C])
    w_stack = sb("w_stack", [P, 4, QUADS, 4, 32])
    w_hi = sb("w_hi", [P, 4, QUADS, 4, 32], F32R)
    w_lo = sb("w_lo", [P, 4, QUADS, 4, 32], F32R)
    vw = sb("vw", [P, H * DV])
    vw_hi = sb("vw_hi", [P, H * DV], F32R)
    vw_lo = sb("vw_lo", [P, H * DV], F32R)
    cw = sb("cw", [P, 2, C])
    lam_in = sb("lam_in", [P, 4, H * HS])
    lam_prod = sb("lam_prod", [P, 2, H * HS])
    lam_sum = sb("lam_sum", [P, 2, H])
    neg_lam = sb("neg_lam", [P, H])
    pat_row = sb("pat_row", [1, 5, P])
    one = sb("one", [1, 1])
    pat = sb("pat", [P, 5])
    x_in = sb("x_in", [P, NQT, C])
    x_res = sb("x_res", [P, NQT, C])
    xT_hi = sb("xT_hi", [P, T], F32R)
    xT_lo = sb("xT_lo", [P, T], F32R)
    rounded = sb("rounded", [P, 4, 2 * T], F32R)
    q_stack = [sb(f"q_stack{i}", [P, 2, 2, T], F32R) for i in range(2)]
    k_stack = [sb(f"k_stack{i}", [P, 2, 2, T], F32R) for i in range(2)]
    q_diag = [sb(f"q_diag{i}", [P, 2, UNITS, 2 * T], F32R) for i in range(2)]
    k_diag = [sb(f"k_diag{i}", [P, 2, UNITS, 2 * T], F32R) for i in range(2)]
    maxima = sb("maxima", [P, NQT, 2, 2, P])
    v_aug = sb("v_aug", [P, NQT, H, 32])
    probs = [sb(f"probs{i}", [P, ITEMS, 512]) for i in range(2)]
    y_sb = sb("y_sb", [P, 2, 2, T])
    y_rden = sb("y_rden", [P, QUADS, 2, NQT, 4])
    y_norm = sb("y_norm", [P, 2, NQT, H, DV])
    y_diff = sb("y_diff", [P, NQT * H, DV])
    y_cent = sb("y_cent", [P, NQT * H, DV])
    y_sq = sb("y_sq", [P, NQT * H, DV])
    y_sum = sb("y_sum", [P, NQT * H])
    y_mean = sb("y_mean", [P, NQT * H])
    y_var = sb("y_var", [P, NQT * H])
    y_rstd = sb("y_rstd", [P, NQT * H])
    y_out = sb("y_out", [P, NQT, H * DV])
    yT = sb("yT", [P, NQT, 2, P])
    z = sb("z", [P, NQT, C])
    z_stats = sb("z_stats", [P, NQT, 6])
    z_mv = sb("z_mv", [P, NQT, 2])
    z_veps = sb("z_veps", [P, NQT])
    z_rstd = sb("z_rstd", [P, NQT])
    neg_half = sb("neg_half", [P, NQT * H])
    x1 = sb("x1", [P, NQT, C])

    max_bank, exp_bank, t_bank = (banks[0], banks[1], banks[4]), banks[2:4], banks[7]
    proj_bank = banks[5:7]
    x_bank = proj_bank[1]
    y_bank = (t_bank, max_bank[2])
    shift_bank = exp_bank
    yt_bank = ((proj_bank[0], t_bank), (t_bank, proj_bank[0]))

    weights_in = sem("weights_in")
    lam_loaded = sem("lam_loaded")
    setup_pool = sem("setup_pool")
    setup_dve = sem("setup_dve")
    lam_exp = sem("lam_exp")
    pat_ready = sem("pat_ready")
    consts_ready = sem("consts_ready")
    x_in_loaded = sem("x_in_loaded")
    x_res_loaded = sem("x_res_loaded")
    xT_ready = sem("xT_ready")
    xT_hi_done = sem("xT_hi_done")
    xT_saved = sem("xT_saved")
    proj_ready = sem("proj_ready")
    round_done = sem("round_done")
    stack_done = sem("stack_done")
    diag_zeroed = sem("diag_zeroed")
    k_diag_in = [sem(f"k_diag_in{u}") for u in range(UNITS)]
    q_diag_in = [sem(f"q_diag_in{u}") for u in range(UNITS)]
    v_ready = sem("v_ready")
    v_saved = sem("v_saved")
    max_ready = sem("max_ready")
    max_done = sem("max_done")
    shift_ready = sem("shift_ready")
    shift_done = sem("shift_done")
    exp_ready = sem("exp_ready")
    exp_done = sem("exp_done")
    masked = sem("masked")
    y_ready = sem("y_ready")
    y_saved = sem("y_saved")
    yt_ready = sem("yt_ready")
    y_scaled = sem("y_scaled")
    dve_step = sem("dve_step")
    waits_passed = sem("waits_passed")
    pool_step = sem("pool_step")
    z_counted = sem("z_counted")
    sum_done = sem("sum_done")
    diff_done = sem("diff_done")
    sq_done = sem("sq_done")
    var_done = sem("var_done")
    heads_done = sem("heads_done")
    nT_ready = sem("nT_ready")
    nT_saved = sem("nT_saved")
    cw_ready = sem("cw_ready")
    z_done = sem("z_done")
    mv_done = sem("mv_done")
    veps_done = sem("veps_done")
    rstd_done = sem("rstd_done")
    x1_done = sem("x1_done")
    x1_stored = sem("x1_stored")

    tiled = lambda a: a.rearrange("b (t p) c -> b p t c", p=P)
    x_t = tiled(t["x"])
    LAM_SUM = 19

    def wait_apart(eng, s, value):
        eng.wait_ge(s, value)
        eng.sem_inc(waits_passed, 1)

    def wait(eng, s, value):
        if not isinstance(value, int) or value > 0:
            eng.wait_ge(s, value)

    def loop(eng, iteration):
        iteration(0, True, False)
        with eng.Fori(1, B - 1) as n:
            iteration(n, True, True)
        iteration(B - 1, True, True)
        iteration(B, False, True)

    blk = nc.Block()
    with blk as block:

        @block.sync
        def _(sp):
            sp.sem_inc(x1_stored, 16)
            sp.sem_inc(z_done, 1)
            for i, name in enumerate(("q1_w", "q2_w", "k1_w", "k2_w")):
                sp.dma_start(w_raw[:, i, :], t[name]).then_inc(weights_in, 16)
            sp.dma_start(vw[:], t["v_w"]).then_inc(weights_in, 16)
            sp.dma_start(cw[:], t["c_w"].rearrange("(k p) n -> p k n", p=P)).then_inc(weights_in, 16)
            for i, lam in enumerate(t["lambdas"]):
                row = lam.rearrange("(o h) d -> o (h d)", o=1)
                sp.dma_start(lam_in[:, i, :], row.broadcast_to([P, H * HS])).then_inc(lam_loaded, 16)
            sp.dma_start(x_in[:], x_t[0]).then_inc(x_in_loaded, 16)

            def spread(stacks, diags, arrived, g):
                for u in range(UNITS):
                    r = slice(32 * u, 32 * u + 32)
                    sp.dma_start(diags[g][r, :, u, :].bitcast(F32),
                                 stacks[g][r].rearrange("p a m t -> p a (m t)").bitcast(F32)
                                 ).then_inc(arrived[u], 16)

            def store_x1(n):
                sp.wait_ge(x1_done, n - 1)
                sp.dma_start(t["x1"][n - 2], x1[:]).then_inc(x1_stored, 16)

            sp.wait_ge(diag_zeroed, 4)
            sp.wait_ge(stack_done, 2)
            spread(k_stack, k_diag, k_diag_in, 0)

            def iteration(n, start, end):
                if end and not (isinstance(n, int) and n < 2):
                    store_x1(n)
                if start and (not isinstance(n, int) or n < B - 1):
                    sp.wait_ge(xT_ready, n + 1)
                    sp.dma_start(x_in[:], x_t[n + 1]).then_inc(x_in_loaded, 16)
                if end:
                    sp.wait_ge(z_done, n)
                    sp.dma_start(x_res[:], x_t[n - 1]).then_inc(x_res_loaded, 16)
                for g in range(OCT):
                    o = OCT * n + g
                    more = start and (g == 0 or not isinstance(n, int) or n < B - 1)
                    if start:
                        sp.wait_ge(shift_done, 2 * o + 2)
                        spread(q_stack, q_diag, q_diag_in, g)
                    if more:
                        sp.wait_ge(stack_done, 4 * (o + 1) + 2)
                        spread(k_stack, k_diag, k_diag_in, 1 - g)

            iteration(0, True, False)
            iteration(1, True, True)
            with sp.Fori(2, B - 1) as n:
                iteration(n, True, True)
            iteration(B - 1, True, True)
            iteration(B, False, True)
            store_x1(B + 1)
            sp.wait_ge(x1_stored, 16 * (B + 1))

        @block.gpsimd
        def _(pool):
            nc.gpsimd.memset(ident[:], 0.0).then_inc(setup_pool, 1)
            nc.gpsimd.memset(causal[:], 0.0).then_inc(setup_pool, 1)
            nc.gpsimd.memset(neg_half[:], -0.5).then_inc(setup_pool, 1)
            pool.wait_ge(setup_pool, 3)
            nc.gpsimd.affine_select(out=ident[:], in_=ident[:], compare_op=ALU.not_equal, fill=1.0,
                                    base=0, pattern=[[-1, P]], channel_multiplier=1).then_inc(setup_pool, 1)
            nc.gpsimd.affine_select(out=causal[:], in_=causal[:], compare_op=ALU.is_ge, fill=NEG,
                                    base=0, pattern=[[-1, P]], channel_multiplier=1).then_inc(setup_pool, 1)
            for d in (*q_diag, *k_diag):
                nc.gpsimd.memset(d[:].bitcast(F32), 0.0).then_inc(diag_zeroed, 1)
            pool.wait_ge(setup_pool, 5)
            nc.gpsimd.tensor_copy(ident_bf[:], ident[:]).then_inc(consts_ready, 1)

            def mask(o, g, items):
                for j in items:
                    wait_apart(pool, exp_done, ITEMS * o + j + 1)
                    if j % 3 == 2:
                        v = probs[g][:, j, :].rearrange("p (a q) -> p a q", q=P)
                    else:
                        v = probs[g][:, j, :].rearrange("p (a q) -> p a q", q=T)[:, :, 0:P]
                    nc.gpsimd.affine_select(out=v, in_=v, compare_op=ALU.is_ge, fill=0.0, base=0,
                                            pattern=[[0, v.shape[1]], [1, P]],
                                            channel_multiplier=-1).then_inc(masked, 1)

            bc = lambda a: a[:].unsqueeze(2).broadcast_to([P, NQT * H, DV])

            def centre_heads(n):
                wait_apart(pool, sum_done, n)
                nc.gpsimd.tensor_scalar(y_mean[:], y_sum[:], 1.0 / DV, None, ALU.mult).then_inc(pool_step, 1)
                pool.wait_ge(pool_step, 4 * (n - 1) + 1)
                nc.gpsimd.tensor_sub(y_cent[:], y_diff[:], bc(y_mean)).then_inc(pool_step, 1)
                pool.wait_ge(pool_step, 4 * (n - 1) + 2)
                nc.gpsimd.tensor_mul(y_sq[:], y_cent[:], y_cent[:]).then_inc(sq_done, 1)

            def scale_heads(n):
                wait_apart(pool, var_done, n)
                nc.gpsimd.tensor_scalar(y_rstd[:], y_var[:], 1.0 / (DV * KEEP * KEEP), EPS / (KEEP * KEEP),
                                        ALU.mult, ALU.add).then_inc(pool_step, 1)
                pool.wait_ge(pool_step, 4 * (n - 1) + 3)
                nc.gpsimd.tensor_tensor(y_mean[:], y_rstd[:], neg_half[:], ALU.pow).then_inc(pool_step, 1)
                pool.wait_ge(pool_step, 4 * (n - 1) + 4)
                nc.gpsimd.tensor_mul(y_out[:].rearrange("p t (h d) -> p (t h) d", d=DV), y_cent[:],
                                     bc(y_mean)).then_inc(heads_done, 1)

            def residual_rstd(n):
                wait_apart(pool, mv_done, n)
                nc.gpsimd.tensor_scalar(z_veps[:], z_mv[:, :, 1], EPS, None, ALU.add).then_inc(veps_done, 1)
                pool.wait_ge(veps_done, n)
                nc.gpsimd.tensor_tensor(z_rstd[:], z_veps[:], neg_half[:, 0:NQT], ALU.pow).then_inc(rstd_done, 1)

            def iteration(n, start, end):
                for g in range(OCT):
                    o = OCT * n + g
                    cur, old = start, (end if g == 0 else start)
                    if old:
                        mask(o - 1, 1 - g, range(EARLY, ITEMS))
                    if g == 1 and end:
                        scale_heads(n)
                    if cur:
                        mask(o, g, range(EARLY // 2))
                    if g == 1 and end:
                        residual_rstd(n)
                    if cur:
                        mask(o, g, range(EARLY // 2, EARLY))
                    if g == 0 and end:
                        centre_heads(n)

            loop(pool, iteration)

        @block.scalar
        def _(act):
            act.wait_ge(setup_dve, LAM_SUM)
            nc.scalar.activation(lam_sum[:], lam_sum[:], ACT.Exp).then_inc(lam_exp, 1)
            act.wait_ge(pat_ready, 2)

            def round_proj(o, j):
                act.wait_ge(proj_ready, 4 * o + j + 1)
                if j < 2:
                    nc.scalar.activation(rounded[:, j, :], proj_bank[j][:], ACT.Identity, scale=pat[:, 3:4],
                                         bias=pat[:, 4:5]).then_inc(round_done, 1)
                else:
                    nc.scalar.activation(rounded[:, j, :], proj_bank[j % 2][:], ACT.Copy,
                                         scale=pat[:, 1:2]).then_inc(round_done, 1)

            def save_y(o, q):
                act.wait_ge(y_ready, 2 * o + q + 1)
                nc.scalar.activation(y_sb[:, q].rearrange("p m t -> p (m t)"), y_bank[q][:],
                                     ACT.Copy).then_inc(y_saved, 1)

            def save_v(n):
                act.wait_ge(v_ready, n + 1)
                nc.scalar.activation(v_aug[:, :, :, 0:DV],
                                     x_bank[:].rearrange("p (t h d) -> p t h d", t=NQT, d=DV),
                                     ACT.Copy).then_inc(v_saved, 1)

            for j in range(4):
                round_proj(0, j)

            def exponentials(o, g, items):
                for j in items:
                    act.wait_ge(exp_ready, ITEMS * o + j + 1)
                    nc.scalar.activation(probs[g][:, j, :], exp_bank[j % 2][:], ACT.Exp,
                                         scale=SCALE).then_inc(exp_done, 1)

            def iteration(n, start, end):
                for g in range(OCT):
                    o = OCT * n + g
                    cur, old = start, (end if g == 0 else start)
                    more = start and (g == 0 or not isinstance(n, int) or n < B - 1)
                    if old:
                        exponentials(o - 1, 1 - g, range(EARLY, EARLY + 3))
                    if g == 1 and start:
                        save_v(n)
                    if old:
                        exponentials(o - 1, 1 - g, range(EARLY + 3, ITEMS))
                    if more:
                        round_proj(o + 1, 0)
                        round_proj(o + 1, 1)
                    if old:
                        save_y(o - 1, 0)
                        save_y(o - 1, 1)
                    if more:
                        round_proj(o + 1, 2)
                        round_proj(o + 1, 3)
                    if g == 1 and end:
                        act.wait_ge(nT_ready, n)
                        nc.scalar.activation(yT[:].rearrange("p t k q -> p (t k q)"), t_bank[:],
                                             ACT.Copy).then_inc(nT_saved, 1)
                    if cur:
                        exponentials(o, g, range(EARLY))

            loop(act, iteration)

        @block.vector
        def _(dve):
            chain = [0]

            def link(ins):
                chain[0] += 1
                ins.then_inc(setup_dve, 1)
                dve.wait_ge(setup_dve, chain[0])

            rows = pat_row[:].rearrange("o k (r c) -> o k r c", c=32)
            link(nc.vector.memset(pat_row[:], 0.0))
            link(nc.vector.memset(rows[:, 0, :, HS:2 * HS], 1.0))
            link(nc.vector.memset(pat_row[:, 1, :], 1.0))
            link(nc.vector.memset(rows[:, 1, :, HS:2 * HS], -1.0))
            link(nc.vector.memset(rows[:, 2, :, 2 * HS:3 * HS], 1.0))
            link(nc.vector.memset(pat_row[:, 3, :], 1.0))
            link(nc.vector.memset(rows[:, 3, :, 2 * HS:3 * HS], -1.0))
            link(nc.vector.memset(rows[:, 4, :, 3 * HS:3 * HS + 1], -1.0))
            nc.vector.memset(one[:], 1.0).then_inc(pat_ready, 1)
            link(nc.vector.memset(w_stack[:], 0.0))
            nc.vector.memset(maxima[:], 0.0)
            link(nc.vector.memset(v_aug[:], 0.0))
            link(nc.vector.memset(v_aug[:, :, :, DV:DV + 1], 1.0))
            dve.wait_ge(weights_in, 96)
            for i in range(4):
                for r in range(3):
                    last = nc.vector.tensor_copy(
                        w_stack[:, i].rearrange("p a b c -> p (a b) c")[:, :, r * HS:(r + 1) * HS],
                        w_raw[:, i, :].rearrange("p (h d) -> p h d", d=HS))
            link(last)
            link(nc.vector.tensor_copy(w_hi[:], w_stack[:]))
            link(nc.vector.tensor_sub(w_lo[:], w_stack[:], w_hi[:]))
            link(nc.vector.tensor_copy(vw_hi[:], vw[:]))
            nc.vector.tensor_sub(vw_lo[:], vw[:], vw_hi[:]).then_inc(consts_ready, 1)
            dve.wait_ge(lam_loaded, 64)
            for i in range(2):
                link(nc.vector.tensor_mul(lam_prod[:, i, :], lam_in[:, 2 * i, :], lam_in[:, 2 * i + 1, :]))
                link(nc.vector.reduce_sum(lam_sum[:, i, :],
                                          lam_prod[:, i, :].rearrange("p (h d) -> p h d", d=HS), AX.X))
            dve.wait_ge(lam_exp, 1)
            link(nc.vector.tensor_sub(neg_lam[:], lam_sum[:, 1, :], lam_sum[:, 0, :]))
            link(nc.vector.tensor_scalar_add(neg_lam[:], neg_lam[:], -LAMBDA_INIT))
            dve.wait_ge(consts_ready, 3)
            link(nc.vector.tensor_copy(pat[:], t_bank[:, 0:5]))
            nc.vector.memset(one[:], 1.0).then_inc(pat_ready, 1)

            def stack(o, g, j):
                q = j % 2
                src, keep = proj_bank[q], (pat[:, 2:3] if j < 2 else pat[:, 0:1])
                dst = (k_stack if j < 2 else q_stack)[g]
                dve.wait_ge(round_done, 4 * o + j + 1)
                nc.vector.scalar_tensor_tensor(
                    out=dst[:, q].rearrange("p m t -> p (m t)"), in0=src[:], scalar=keep,
                    in1=rounded[:, j, :], op0=ALU.mult, op1=ALU.add).then_inc(stack_done, 1)

            def add_shift(o, g, q):
                dve.wait_ge(shift_ready, 2 * o + q + 1)
                dst = q_stack[g][:, q].rearrange("p m t -> p (m t)")
                nc.vector.tensor_add(dst, shift_bank[q][:], dst).then_inc(shift_done, 1)

            def scale_y(o, g, q):
                quad = 2 * g + q
                dve.wait_ge(yt_ready, 2 * o + q + 1)
                v = yt_bank[g][q][:].rearrange("p (m t h c) -> p m t h c", m=2, t=NQT, c=32)
                nc.vector.reciprocal(y_rden[:, quad], v[:, :, :, :, DV]).then_inc(dve_step, 1)
                dve.wait_ge(dve_step, 4 * o + 2 * q + 1)
                for i in range(NQT):
                    last = nc.vector.tensor_mul(y_rden[:, quad, 1, i], y_rden[:, quad, 1, i],
                                                neg_lam[:, 4 * quad:4 * quad + 4])
                last.then_inc(dve_step, 1)
                dve.wait_ge(dve_step, 4 * o + 2 * q + 2)
                for m in range(2):
                    last = nc.vector.tensor_mul(
                        y_norm[:, m, :, 4 * quad:4 * quad + 4, :], v[:, m, :, :, 0:DV],
                        y_rden[:, quad, m].unsqueeze(3).broadcast_to([P, NQT, 4, DV]))
                last.then_inc(y_scaled, 1)

            def save_xT(n):
                dve.wait_ge(xT_ready, n + 1)
                nc.vector.tensor_copy(xT_hi[:], x_bank[:, 0:T]).then_inc(xT_hi_done, 1)
                dve.wait_ge(xT_hi_done, n + 1)
                nc.vector.tensor_sub(xT_lo[:], x_bank[:, 0:T], xT_hi[:]).then_inc(xT_saved, 1)

            save_xT(0)
            for j in range(4):
                stack(0, 0, j)

            def maximum(o, g, j):
                row = 32 * (j // 3) + 3 * HS
                dve.wait_ge(max_ready, ITEMS * o + j + 1)
                src = max_bank[j % 3][:]
                if j % 3 == 2:
                    dst = maxima[:, 0, :, :, row]
                    src = src.rearrange("p (a m k) -> p a m k", a=2, k=P)
                else:
                    dst = maxima[:, 1, j % 3, :, row]
                    src = src.rearrange("p (m k) -> p m k", k=T)
                nc.vector.reduce_max(dst, src, AX.X).then_inc(max_done, 1)

            def residual(n):
                dve.wait_ge(cw_ready, n)
                dve.wait_ge(x_res_loaded, 16 * n)
                nc.vector.tensor_add(z[:], t_bank[:, 0:NQT * C].rearrange("p (t c) -> p t c", t=NQT),
                                     x_res[:]).then_inc(z_done, 1)
                dve.wait_ge(z_done, n + 1)
                for i in range(NQT):
                    last = nc.vector.bn_stats(z_stats[:, i, :], z[:, i, :])
                last.then_inc(z_counted, 1)
                wait_apart(dve, z_counted, n)
                for i in range(NQT):
                    last = nc.vector.bn_aggr(z_mv[:, i, :], z_stats[:, i, :])
                last.then_inc(mv_done, 1)

            half = lambda i: y_norm[:, i].rearrange("p t h d -> p (t h) d")

            def sum_heads(n):
                dve.wait_ge(y_scaled, 4 * n)
                nc.vector.tensor_add(y_diff[:], half(0), half(1)).then_inc(diff_done, 1)
                dve.wait_ge(diff_done, n)
                nc.vector.reduce_sum(y_sum[:], y_diff[:], AX.X).then_inc(sum_done, 1)

            def normalize(n):
                dve.wait_ge(rstd_done, n)
                dve.wait_ge(x1_stored, 16 * n)
                for i in range(NQT):
                    last = nc.vector.tensor_scalar(x1[:, i, :], z[:, i, :], z_mv[:, i, 0:1],
                                                   z_rstd[:, i:i + 1], ALU.subtract, ALU.mult)
                last.then_inc(x1_done, 1)

            def iteration(n, start, end):
                for g in range(OCT):
                    o = OCT * n + g
                    cur, old = start, (end if g == 0 else start)
                    more = start and (g == 0 or not isinstance(n, int) or n < B - 1)
                    for j in range(ITEMS):
                        if cur:
                            maximum(o, g, j)
                        if j == 3 and g == 0 and end and not (isinstance(n, int) and n < 2):
                            normalize(n - 1)
                        if j == 3 and g == 1 and end:
                            dve.wait_ge(sq_done, n)
                            nc.vector.reduce_sum(y_var[:], y_sq[:], AX.X).then_inc(var_done, 1)
                        if j == ITEMS // 2 and g == 1 and more:
                            save_xT(n + 1)
                    if cur:
                        add_shift(o, g, 0)
                        add_shift(o, g, 1)
                    if more:
                        for j in range(4):
                            stack(o + 1, 1 - g, j)
                    if old:
                        scale_y(o - 1, 1 - g, 0)
                    if g == 1 and end:
                        residual(n)
                    if old:
                        scale_y(o - 1, 1 - g, 1)
                    if g == 0 and end:
                        sum_heads(n)

            iteration(0, True, False)
            iteration(1, True, True)
            with dve.Fori(2, B - 1) as n:
                iteration(n, True, True)
            iteration(B - 1, True, True)
            iteration(B, False, True)
            normalize(B)

        @block.tensor
        def _(pe):
            mm = nc.tensor.matmul
            pe.wait_ge(pat_ready, 1)
            for i in range(5):
                last = mm(t_bank[:, i:i + 1], pat_row[0:1, i, :], one[0:1, 0:1], start=True, stop=True)
            last.then_inc(consts_ready, 1)
            pe.wait_ge(consts_ready, 3)

            def transpose_x(n):
                pe.wait_ge(x_in_loaded, 16 * (n + 1))
                wait(pe, v_saved, n)
                for i in range(NQT):
                    last = nc.tensor.transpose(x_bank[:, i * P:(i + 1) * P], x_in[:, i, :], ident[:])
                last.then_inc(xT_ready, 1)

            def product3(dst, a_hi, a_lo, b_hi, b_lo, first):
                mm(dst, a_lo, b_hi, start=first, stop=False, skip_group_check=True)
                mm(dst, a_hi, b_lo, start=False, stop=False, skip_group_check=True)
                return mm(dst, a_hi, b_hi, start=False, stop=True, skip_group_check=True)

            def project(o, g, j):
                quad = 2 * g + j % 2
                bank, m0 = proj_bank[j % 2], (2 if j < 2 else 0)
                wait(pe, stack_done, 4 * o + j - 1)
                for m in range(2):
                    hi, lo = (w[:, m0 + m, quad].rearrange("p a c -> p (a c)") for w in (w_hi, w_lo))
                    last = product3(bank[:, m * T:(m + 1) * T], hi, lo, xT_hi[:], xT_lo[:], m == 0)
                last.then_inc(proj_ready, 1)

            def values(n):
                for i in range(NQT):
                    r = slice(i * P, (i + 1) * P)
                    last = product3(x_bank[:, i * T:(i + 1) * T], xT_hi[:, r], xT_lo[:, r], vw_hi[:], vw_lo[:],
                                    i == 0)
                last.then_inc(v_ready, 1)

            def max_scores(o, g, j):
                u, kind = j // 3, j % 3
                bank = max_bank[kind]
                if j == 0:
                    pe.wait_ge(stack_done, 4 * (o + 1))
                if kind == 0:
                    pe.wait_ge(k_diag_in[u], 16 * (o + 1))
                wait(pe, max_done, ITEMS * o + j - 2)
                parts = [(kind, m, 1, T) for m in range(2)] if kind < 2 else \
                        [(a, m, 0, P) for a in range(2) for m in range(2)]
                at = 0
                for k, (a, m, qt, w) in enumerate(parts):
                    mm(bank[:, at:at + w], q_stack[g][:, a, m, qt * P:(qt + 1) * P],
                       k_diag[g][:, a, u, m * T:m * T + w],
                       start=(k == 0), stop=False, skip_group_check=True)
                    at += w
                if kind < 2:
                    dst = bank[:].rearrange("p (m k) -> p m k", k=T)[:, :, P:T]
                else:
                    dst = bank[:].rearrange("p (m k) -> p m k", k=P)
                mask = causal[:].unsqueeze(1).broadcast_to([P, dst.shape[1], P])
                mm(dst, ident_bf[:], mask, start=False, stop=True, skip_group_check=True).then_inc(max_ready, 1)

            def exp_scores(o, g, j):
                u, kind = j // 3, j % 3
                bank = exp_bank[j % 2]
                if kind == 0:
                    pe.wait_ge(q_diag_in[u], 16 * (o + 1))
                wait(pe, exp_done, ITEMS * o + j - 1)
                parts = [(kind, m, 0, 0, T) for m in range(2)] if kind < 2 else \
                        [(a, m, 1, P, P) for a in range(2) for m in range(2)]
                at = 0
                for k, (a, m, kt, q0, w) in enumerate(parts):
                    last = mm(bank[:, at:at + w], k_stack[g][:, a, m, kt * P:(kt + 1) * P],
                              q_diag[g][:, a, u, m * T + q0:m * T + q0 + w], start=(k == 0), stop=(k == len(parts) - 1),
                              skip_group_check=True)
                    at += w
                last.then_inc(exp_ready, 1)

            def shift(o, q):
                if q == 0:
                    pe.wait_ge(max_done, ITEMS * (o + 1))
                    wait(pe, exp_done, ITEMS * o)
                for m in range(2):
                    for i in range(NQT):
                        last = nc.tensor.transpose(shift_bank[q][:, (2 * m + i) * P:(2 * m + i + 1) * P],
                                                   maxima[:, i, q, m, :], ident[:])
                last.then_inc(shift_ready, 1)

            def attend(o, g, q, m):
                if q == 0 and m == 0:
                    pe.wait_ge(masked, ITEMS * (o + 1))
                    wait(pe, y_saved, 2 * o)
                    wait(pe, y_scaled, 2 * o)
                quad = 2 * g + q
                for kt in range(NQT):
                    for u in range(UNITS):
                        if kt == 0:
                            rhs, q0, w = probs[g][:, 3 * u + q, m * T:(m + 1) * T], 0, T
                        else:
                            c = (2 * q + m) * P
                            rhs, q0, w = probs[g][:, 3 * u + 2, c:c + P], P, P
                        last = mm(y_bank[q][32 * u:32 * u + 32, m * T + q0:m * T + q0 + w],
                                  v_aug[:, kt, 4 * quad + u, :], rhs, start=(kt == 0), stop=(kt == 1))
                if m == 1:
                    last.then_inc(y_ready, 1)

            def transpose_y(o, g, q):
                wait(pe, y_scaled, 2 * o)
                pe.wait_ge(y_saved, 2 * o + q + 1)
                for m in range(2):
                    for i in range(NQT):
                        last = nc.tensor.transpose(yt_bank[g][q][:, (2 * m + i) * P:(2 * m + i + 1) * P],
                                                   y_sb[:, q, m, i * P:(i + 1) * P], ident[:])
                last.then_inc(yt_ready, 1)

            transpose_x(0)
            pe.wait_ge(xT_saved, 1)
            for j in range(4):
                project(0, 0, j)

            def transpose_heads(n):
                pe.wait_ge(heads_done, n)
                for i in range(NQT):
                    for k in range(2):
                        last = nc.tensor.transpose(t_bank[:, (2 * i + k) * P:(2 * i + k + 1) * P],
                                                   y_out[:, i, k * P:(k + 1) * P], ident[:])
                last.then_inc(nT_ready, 1)

            def project_out(n):
                pe.wait_ge(nT_saved, n)
                for i in range(NQT):
                    for k in range(2):
                        last = mm(t_bank[:, i * C:(i + 1) * C], yT[:, i, k, :], cw[:, k, :],
                                  start=(k == 0), stop=(k == 1))
                last.then_inc(cw_ready, 1)

            def iteration(n, start, end):
                for g in range(OCT):
                    o = OCT * n + g
                    cur, old = start, (end if g == 0 else start)
                    more = start and (g == 0 or not isinstance(n, int) or n < B - 1)
                    for j in range(ITEMS):
                        if cur:
                            max_scores(o, g, j)
                        if old and EARLY + j < ITEMS:
                            exp_scores(o - 1, 1 - g, EARLY + j)
                        if g == 1 and start and j == 2:
                            values(n)
                        if g == 1 and more and j == ITEMS // 2:
                            transpose_x(n + 1)
                        if more and j == 9:
                            if g == 1:
                                pe.wait_ge(xT_saved, n + 2)
                            wait(pe, y_scaled, 2 * (o - 1))
                            project(o + 1, 1 - g, 0)
                        if more and j == 11:
                            project(o + 1, 1 - g, 1)
                    if g == 1 and old:
                        pe.wait_ge(v_saved, n + 1)
                    if old:
                        attend(o - 1, 1 - g, 0, 0)
                        attend(o - 1, 1 - g, 0, 1)
                    if cur:
                        shift(o, 0)
                        shift(o, 1)
                    if old:
                        attend(o - 1, 1 - g, 1, 0)
                        attend(o - 1, 1 - g, 1, 1)
                    if g == 0 and old:
                        transpose_y(o - 1, 1, 0)
                    if more:
                        project(o + 1, 1 - g, 2)
                        project(o + 1, 1 - g, 3)
                    if cur:
                        pe.wait_ge(shift_done, 2 * o + 2)
                    if g == 1 and end:
                        if old:
                            pe.wait_ge(y_saved, 2 * o - 1)
                        transpose_heads(n)
                    for j in range(EARLY):
                        if old and j == 1:
                            if more:
                                pe.wait_ge(stack_done, 4 * (o + 1) + 3)
                            transpose_y(o - 1, 1 - g, 1 - g)
                        if g == 1 and end and j == 2:
                            project_out(n)
                        if cur:
                            exp_scores(o, g, j)
                    if g == 1 and old:
                        if end:
                            pe.wait_ge(z_done, n + 1)
                        transpose_y(o - 1, 0, 1)

            loop(pe, iteration)


def feed_forward(nc, sb, sem, banks, ident, t):
    NE = E + 1
    CH = NE * HC
    PG = GT // T
    PAIRS = NG // 2
    SLOTS = 3
    gate_w = sb("gate_w", [P, E])
    gate_b = sb("gate_b", [P, E])
    ffn_w_raw = sb("ffn_w_raw", [P, NE, 2, HID])
    w1_hi = sb("w1_hi", [P, NE, HID], F32R)
    w1_lo = sb("w1_lo", [P, NE, HID], F32R)
    w2_hi = sb("w2_hi", [P, NE, HC * C], F32R)
    w2_lo = sb("w2_lo", [P, NE, HC * C], F32R)
    bias_rows = sb("bias_rows", [CH + NE, P])
    bias = sb("bias", [P, CH + NE])
    xg = [sb(f"xg{i}", [P, TT, C]) for i in range(2)]
    xt = sb("xt", [P, GT])
    x_hi = [sb(f"x_hi{i}", [P, GT], F32R) for i in range(2)]
    x_lo = [sb(f"x_lo{i}", [P, GT], F32R) for i in range(2)]
    logits = sb("logits", [P, TT, E])
    rest = sb("rest", [P, TT, E])
    hit = sb("hit", [P, TT, E])
    first = sb("first", [P, TT, E])
    second = sb("second", [P, TT, E])
    comb = sb("comb", [P, TT, E])
    rev = sb("rev", [P, E])
    top1 = sb("top1", [P, TT])
    top2 = sb("top2", [P, TT])
    rank = sb("rank", [P, TT])
    gap = sb("gap", [P, TT])
    wt1 = sb("wt1", [P, TT])
    wt2 = sb("wt2", [P, TT])
    comb_rows = sb("comb_rows", [TT * E, P])
    comb_all = [sb(f"comb_all{i}", [P, TT, E, P]) for i in range(2)]
    h = [sb(f"h{i}", [P, GT]) for i in range(SLOTS)]
    h_hi = [sb(f"h_hi{i}", [P, GT], F32R) for i in range(SLOTS)]
    h_lo = [sb(f"h_lo{i}", [P, GT], F32R) for i in range(SLOTS)]
    acc = [sb(f"acc{i}", [P, GT]) for i in range(2)]
    weighted = [sb(f"weighted{i}", [P, GT]) for i in range(2)]
    res = sb("res", [P, TT, C])
    stats = sb("stats", [P, TT, 6])
    mv = sb("mv", [P, TT, 2])
    veps = sb("veps", [P, TT])
    rstd = sb("rstd", [P, TT])
    minus_half = sb("minus_half", [P, TT])
    out_sb = sb("out_sb", [P, TT, C])
    comb_dram = nc.dram_tensor("comb_dram", [2, TT * E, P], F32, kind="Internal").ap()

    up_bank, down_bank = banks[0:SLOTS], banks[3:5]
    xt_bank, gate_bank, out_bank = banks[5], banks[6], banks[7]

    gate_loaded = sem("gate_loaded")
    bias_turned = sem("bias_turned")
    bias_saved = sem("bias_saved")
    w_loaded = [sem(f"w_loaded{e}") for e in range(NE)]
    w_high = sem("w_high")
    w_split = sem("w_split")
    xg_loaded = [sem(f"xg_loaded{i}") for i in range(2)]
    xt_ready = sem("xt_ready")
    xt_saved = sem("xt_saved")
    xh_done = sem("xh_done")
    x_split = sem("x_split")
    logits_ready = sem("logits_ready")
    gate_step = sem("gate_step")
    gap_done = sem("gap_done")
    gap_tanh = sem("gap_tanh")
    comb_done = sem("comb_done")
    comb_turned = sem("comb_turned")
    comb_saved = sem("comb_saved")
    comb_stored = sem("comb_stored")
    comb_in = [sem(f"comb_in{i}") for i in range(2)]
    ffn_consts = sem("ffn_consts")
    up_ready = sem("up_ready")
    gelu_done = sem("gelu_done")
    hi_done = sem("hi_done")
    hi_own = sem("hi_own")
    lo_done = sem("lo_done")
    down_done = sem("down_done")
    down_read = sem("down_read")
    added = sem("added")
    out_turned = sem("out_turned")
    res_done = sem("res_done")
    res_counted = sem("res_counted")
    group_mv = sem("group_mv")
    group_veps = sem("group_veps")
    group_rstd = sem("group_rstd")
    out_done = sem("out_done")
    out_stored = sem("out_stored")
    waits_passed = sem("ffn_waits_passed")

    x1_v = t["x1"]
    out_v = t["out"].rearrange("b (t p) c -> b p t c", p=P)

    def wait(eng, s, value):
        if not isinstance(value, int) or value > 0:
            eng.wait_ge(s, value)

    def loop(eng, body):
        body(0, True, False)
        with eng.Fori(1, PAIRS - 1) as i:
            body(i, False, False)
        body(PAIRS - 1, False, True)

    with nc.Block() as block:

        @block.sync
        def _(sp):
            def load_group(g, p):
                sp.dma_start(xg[p][:].rearrange("p (b t) c -> p b t c", b=PG),
                             x1_v[bass.ds(g * PG, PG)].rearrange("b p t c -> p b t c")
                             ).then_inc(xg_loaded[p], 16)

            def spread_comb(g, p):
                sp.wait_ge(comb_saved, g + 1)
                sp.dma_start(comb_dram[p], comb_rows[:]).then_inc(comb_stored, 16)
                sp.wait_ge(comb_stored, 16 * (g + 1))
                sp.sem_inc(waits_passed, 1)
                wait(sp, down_read, NE * (g - 1))
                row = comb_dram[p].rearrange("(o r) q -> o (r q)", o=1)
                sp.dma_start(comb_all[p][:].rearrange("p t e q -> p (t e q)"),
                             row.broadcast_to([P, TT * E * P])).then_inc(comb_in[p], 16)

            load_group(0, 0)
            sp.dma_start(gate_w[:], t["gate_w"]).then_inc(gate_loaded, 16)
            sp.dma_start(gate_b[:], t["gate_b"].rearrange("(o e) -> o e", o=1).broadcast_to([P, E])
                         ).then_inc(gate_loaded, 16)
            sp.dma_start(bias_rows[0:HC, :], t["bs1"].rearrange("(k p) -> k p", p=P)).then_inc(gate_loaded, 16)
            sp.dma_start(bias_rows[HC:CH, :], t["b1"].rearrange("e (k p) -> (e k) p", p=P)
                         ).then_inc(gate_loaded, 16)
            sp.dma_start(bias_rows[CH:CH + 1, :], t["bs2"].rearrange("(o c) -> o c", o=1)
                         ).then_inc(gate_loaded, 16)
            sp.dma_start(bias_rows[CH + 1:CH + NE, :], t["b2"]).then_inc(gate_loaded, 16)
            for e in range(NE):
                sp.dma_start(ffn_w_raw[:, e, 0, :], t["ws1"] if e == 0 else t["w1"][e - 1]
                             ).then_inc(w_loaded[e], 16)
                sp.dma_start(ffn_w_raw[:, e, 1, :].rearrange("p (k c) -> p k c", c=C),
                             (t["ws2"] if e == 0 else t["w2"][e - 1]).rearrange("(k p) c -> p k c", p=P)
                             ).then_inc(w_loaded[e], 16)
            load_group(1, 1)
            spread_comb(0, 0)

            def body(i, start, end):
                for p in range(2):
                    g = 2 * i + p
                    if not (end and p == 1):
                        spread_comb(g + 1, 1 - p)
                    if not end:
                        sp.wait_ge(res_done, g + 1)
                        load_group(g + 2, p)
                    sp.wait_ge(out_done, g + 1)
                    sp.dma_start(out_v[bass.ds(g * PG, PG)].rearrange("b p t c -> p b t c"),
                                 out_sb[:].rearrange("p (b t) c -> p b t c", b=PG)).then_inc(out_stored, 16)

            loop(sp, body)
            sp.wait_ge(out_stored, 16 * NG)

        @block.gpsimd
        def _(pool):
            def add(g, p, e):
                pool.wait_ge(down_read, NE * g + e + 1)
                if e > 1:
                    pool.wait_ge(added, E * g + e - 1)
                nc.gpsimd.tensor_add(acc[p][:], acc[p][:], weighted[(e - 1) % 2][:]).then_inc(added, 1)

            nc.gpsimd.memset(minus_half[:], -0.5).then_inc(ffn_consts, 1)
            pool.wait_ge(ffn_consts, 1)
            for e in range(NE):
                for k, (hi, lo) in enumerate(((w1_hi, w1_lo), (w2_hi, w2_lo))):
                    pool.wait_ge(w_high, 2 * e + k + 1)
                    nc.gpsimd.tensor_sub(lo[:, e, :], ffn_w_raw[:, e, k, :], hi[:, e, :]).then_inc(w_split, 1)
                if e >= 2:
                    add(0, 0, e - 1)
            add(0, 0, E)

            def normalize(g):
                pool.wait_ge(group_mv, g + 1)
                pool.sem_inc(waits_passed, 1)
                nc.gpsimd.tensor_scalar(veps[:], mv[:, :, 1], EPS, None, ALU.add).then_inc(group_veps, 1)
                pool.wait_ge(group_veps, g + 1)
                nc.gpsimd.tensor_tensor(rstd[:], veps[:], minus_half[:], ALU.pow).then_inc(group_rstd, 1)
                pool.wait_ge(group_rstd, g + 1)
                pool.sem_inc(waits_passed, 1)
                if not isinstance(g, int) or g > 0:
                    pool.wait_ge(out_stored, 16 * g)
                    pool.sem_inc(waits_passed, 1)
                for k in range(TT):
                    last = nc.gpsimd.tensor_scalar(out_sb[:, k, :], res[:, k, :], mv[:, k, 0:1],
                                                   rstd[:, k:k + 1], ALU.subtract, ALU.mult)
                last.then_inc(out_done, 1)

            def body(i, start, end):
                for p in range(2):
                    g = 2 * i + p
                    if not (start and p == 0):
                        normalize(g - 1)
                        for e in range(1, NE):
                            add(g, p, e)

            loop(pool, body)
            normalize(NG - 1)

        @block.scalar
        def _(act):
            def save_xt(g):
                act.wait_ge(xt_ready, g + 1)
                nc.scalar.activation(xt[:], xt_bank[:], ACT.Copy).then_inc(xt_saved, 1)

            def tanh_gap(g):
                act.wait_ge(gap_done, g + 1)
                nc.scalar.activation(gap[:], gap[:], ACT.Tanh, scale=0.5).then_inc(gap_tanh, 1)

            def save_comb(g):
                act.wait_ge(comb_turned, g + 1)
                wait(act, comb_stored, 16 * g)
                nc.scalar.activation(comb_rows[:], gate_bank[0:TT * E, TT * E:TT * E + P],
                                     ACT.Copy).then_inc(comb_saved, 1)

            def weights_high(e):
                act.wait_ge(w_loaded[e], 32)
                for k, hi in enumerate((w1_hi, w2_hi)):
                    nc.scalar.activation(hi[:, e, :], ffn_w_raw[:, e, k, :], ACT.Copy).then_inc(w_high, 1)

            save_xt(0)
            tanh_gap(0)
            weights_high(0)
            save_comb(0)
            weights_high(1)
            act.wait_ge(bias_saved, 1)

            def body(i, start, end):
                for c in range(2 * CH):
                    p, k = c // CH, c % CH
                    g = 2 * i + p
                    q = 2 * CH * i + c
                    if not (end and p == 1):
                        if k == 18:
                            save_xt(g + 1)
                        if k == 28:
                            tanh_gap(g + 1)
                        if k == 33:
                            save_comb(g + 1)
                    if start and p == 0 and k % HC == 0 and k // HC + 2 < NE:
                        weights_high(k // HC + 2)
                    act.wait_ge(up_ready, q + 1)
                    wait(act, lo_done, q + 1 - SLOTS)
                    nc.scalar.activation(h[c % SLOTS][:], up_bank[c % SLOTS][:], ACT.Gelu,
                                         bias=bias[:, k:k + 1]).then_inc(gelu_done, 1)
                    if c % HC == HC - 1:
                        continue
                    act.wait_ge(gelu_done, q + 1)
                    wait(act, down_done, q + 1 - SLOTS)
                    nc.scalar.activation(h_hi[c % SLOTS][:], h[c % SLOTS][:], ACT.Copy).then_inc(hi_done, 1)

            loop(act, body)

        @block.vector
        def _(dve):
            for k in range(E):
                nc.vector.memset(rev[:, k:k + 1], float(E - k))
            dve.wait_ge(gate_loaded, 96)

            per = lambda a: a[:].unsqueeze(2).broadcast_to([P, TT, E])
            rv = rev[:].unsqueeze(1).broadcast_to([P, TT, E])
            STEPS = 17

            def split_x(g, p):
                dve.wait_ge(xt_saved, g + 1)
                nc.vector.tensor_copy(x_hi[p][:], xt[:]).then_inc(xh_done, 1)
                dve.wait_ge(xh_done, g + 1)
                nc.vector.tensor_sub(x_lo[p][:], xt[:], x_hi[p][:]).then_inc(x_split, 1)

            def step(g, k, *instructions):
                instructions[-1].then_inc(gate_step, 1)
                dve.wait_ge(gate_step, STEPS * g + k)

            def equal_largest(g):
                dve.wait_ge(logits_ready, g + 1)
                step(g, 1, nc.vector.tensor_add(logits[:], gate_bank[:, 0:TT * E].rearrange(
                    "p (t e) -> p t e", e=E), gate_b[:].unsqueeze(1).broadcast_to([P, TT, E])))
                step(g, 2, nc.vector.reduce_max(top1[:], logits[:], AX.X))
                step(g, 3, nc.vector.tensor_tensor(hit[:], logits[:], per(top1), ALU.is_equal))

            def pick_first(g):
                step(g, 4, nc.vector.tensor_mul(hit[:], hit[:], rv))
                step(g, 5, nc.vector.reduce_max(rank[:], hit[:], AX.X))
                step(g, 6, nc.vector.tensor_tensor(first[:], hit[:], per(rank), ALU.is_equal))

            def measure_gap(g):
                flat = lambda a: a[:].rearrange("p t e -> p (t e)")
                step(g, 7, nc.vector.scalar_tensor_tensor(out=flat(rest), in0=flat(first), scalar=NEG,
                                                          in1=flat(logits), op0=ALU.mult, op1=ALU.add))
                step(g, 8, nc.vector.reduce_max(top2[:], rest[:], AX.X))
                nc.vector.tensor_sub(gap[:], top2[:], top1[:]).then_inc(gap_done, 1)

            def pick_second(g):
                step(g, 9, nc.vector.tensor_tensor(hit[:], rest[:], per(top2), ALU.is_equal))
                step(g, 10, nc.vector.tensor_mul(hit[:], hit[:], rv))
                step(g, 11, nc.vector.reduce_max(rank[:], hit[:], AX.X))
                step(g, 12, nc.vector.tensor_tensor(second[:], hit[:], per(rank), ALU.is_equal))

            def weigh(g):
                dve.wait_ge(gap_tanh, g + 1)
                step(g, 13, nc.vector.tensor_scalar(wt1[:], gap[:], -0.5, 0.5, ALU.mult, ALU.add))
                step(g, 14, nc.vector.tensor_scalar(wt2[:], gap[:], 0.5, 0.5, ALU.mult, ALU.add))
                step(g, 15, nc.vector.tensor_mul(first[:], first[:], per(wt1)))
                step(g, 16, nc.vector.tensor_mul(second[:], second[:], per(wt2)))
                step(g, 17, nc.vector.tensor_add(comb[:], first[:], second[:]))
                dve.sem_inc(comb_done, 1)

            split_x(0, 0)
            equal_largest(0)
            pick_first(0)
            measure_gap(0)
            pick_second(0)
            weigh(0)
            dve.wait_ge(bias_turned, 1)
            nc.vector.tensor_copy(bias[:], out_bank[:, 0:CH + NE]).then_inc(bias_saved, 1)
            dve.wait_ge(bias_saved, 1)

            def combine(i, m):
                p, e = (m // NE) % 2, m % NE
                g = 2 * i + m // NE
                src = down_bank[m % 2][:]
                b2 = bias[:, CH + e:CH + e + 1]
                dve.wait_ge(down_done, 2 * CH * i + HC * (m + 1))
                if e == 0:
                    nc.vector.tensor_scalar(acc[p][:], src, b2, None, ALU.add).then_inc(down_read, 1)
                    return
                wait(dve, added, E * g + e - 2)
                if e == 1:
                    dve.wait_ge(comb_in[p], 16 * (i + 1))
                tiles = lambda a: a.rearrange("p (t q) -> p t q", q=P)
                nc.vector.scalar_tensor_tensor(out=tiles(weighted[(e - 1) % 2][:]), in0=tiles(src), scalar=b2,
                                               in1=comb_all[p][:, :, e - 1, :], op0=ALU.add,
                                               op1=ALU.mult).then_inc(down_read, 1)

            def residual(g, p):
                dve.wait_ge(out_turned, g + 1)
                wait(dve, out_done, g)
                nc.vector.tensor_add(res[:], out_bank[:].rearrange("p (t c) -> p t c", c=C),
                                     xg[p][:]).then_inc(res_done, 1)

            def count_residual(g):
                dve.wait_ge(res_done, g + 1)
                for k in range(TT):
                    last = nc.vector.bn_stats(stats[:, k, :], res[:, k, :])
                last.then_inc(res_counted, 1)

            def aggregate(g):
                dve.wait_ge(res_counted, g + 1)
                dve.sem_inc(waits_passed, 1)
                for k in range(TT):
                    last = nc.vector.bn_aggr(mv[:, k, :], stats[:, k, :])
                last.then_inc(group_mv, 1)

            def body(i, start, end):
                for c in range(2 * CH):
                    p, k = c // CH, c % CH
                    g = 2 * i + p
                    q = 2 * CH * i + c
                    if c % HC == 2 and not (start and c == 2):
                        combine(i, (c - 2) // HC - 1)
                    if not (start and p == 0):
                        if k == 8:
                            residual(g - 1, 1 - p)
                        if k == 9:
                            count_residual(g - 1)
                        if k == 11:
                            aggregate(g - 1)
                    if not (end and p == 1):
                        if k == 20:
                            split_x(g + 1, 1 - p)
                        if k == 23:
                            equal_largest(g + 1)
                        if k == 24:
                            pick_first(g + 1)
                        if k == 25:
                            measure_gap(g + 1)
                        if k == 27:
                            pick_second(g + 1)
                        if k == 29:
                            weigh(g + 1)
                    m = c // HC
                    if c % HC == HC - 1:
                        dve.wait_ge(gelu_done, q + 1)
                        wait(dve, down_done, q + 1 - SLOTS)
                        nc.vector.tensor_copy(h_hi[c % SLOTS][:], h[c % SLOTS][:]).then_inc(hi_own, 1)
                        dve.wait_ge(hi_own, 2 * NE * i + m + 1)
                    else:
                        dve.wait_ge(hi_done, (HC - 1) * (2 * NE * i + m) + c % HC + 1)
                    nc.vector.tensor_sub(h_lo[c % SLOTS][:], h[c % SLOTS][:],
                                         h_hi[c % SLOTS][:]).then_inc(lo_done, 1)

            loop(dve, body)
            combine(PAIRS - 1, 2 * NE - 1)
            residual(NG - 1, 1)
            count_residual(NG - 1)
            aggregate(NG - 1)

        @block.tensor
        def _(pe):
            mm = nc.tensor.matmul

            def product3(dst, a_hi, a_lo, b_hi, b_lo, first, last):
                mm(dst, a_lo, b_hi, start=first, stop=False)
                mm(dst, a_hi, b_lo, start=False, stop=False)
                return mm(dst, a_hi, b_hi, start=False, stop=last)

            def turn_x(g, p, i):
                pe.wait_ge(xg_loaded[p], 16 * (i + 1))
                wait(pe, xt_saved, g)
                for k in range(TT):
                    last = nc.tensor.transpose(xt_bank[:, k * P:(k + 1) * P], xg[p][:, k, :], ident[:])
                last.then_inc(xt_ready, 1)

            def gate_logits(g):
                pe.wait_ge(xt_saved, g + 1)
                wait(pe, comb_saved, g)
                for k in range(TT):
                    last = mm(gate_bank[:, k * E:(k + 1) * E], xt[:, k * P:(k + 1) * P], gate_w[:],
                              start=True, stop=True)
                last.then_inc(logits_ready, 1)

            def turn_comb(g):
                pe.wait_ge(comb_done, g + 1)
                nc.tensor.transpose(gate_bank[0:TT * E, TT * E:TT * E + P], comb[:].rearrange("p t e -> p (t e)"),
                                    ident[:]).then_inc(comb_turned, 1)

            def turn_out(g, p):
                pe.wait_ge(added, E * (g + 1))
                wait(pe, res_done, g)
                for k in range(TT):
                    last = nc.tensor.transpose(out_bank[:, k * P:(k + 1) * P], acc[p][:, k * P:(k + 1) * P],
                                               ident[:])
                last.then_inc(out_turned, 1)

            def up(i, c, start):
                p, e, k = (c // CH) % 2, (c % CH) // HC, c % HC
                if c % CH == 0:
                    pe.wait_ge(x_split, 2 * i + c // CH + 1)
                if start and c < CH and k == 0:
                    pe.wait_ge(w_split, 2 * e + 1)
                wait(pe, gelu_done, 2 * CH * i + c + 1 - SLOTS)
                cols = slice(k * P, (k + 1) * P)
                product3(up_bank[c % SLOTS][:], w1_hi[:, e, cols], w1_lo[:, e, cols], x_hi[p][:], x_lo[p][:],
                         True, True).then_inc(up_ready, 1)

            def down(i, c, start):
                m, e, k = c // HC, (c % CH) // HC, c % HC
                if k == 0:
                    wait(pe, down_read, 2 * NE * i + m - 1)
                if start and c < CH and k == 0:
                    pe.wait_ge(w_split, 2 * e + 2)
                pe.wait_ge(lo_done, 2 * CH * i + c + 1)
                cols = slice(k * C, (k + 1) * C)
                product3(down_bank[m % 2][:], w2_hi[:, e, cols], w2_lo[:, e, cols], h_hi[c % SLOTS][:],
                         h_lo[c % SLOTS][:], k == 0, k == HC - 1).then_inc(down_done, 1)

            turn_x(0, 0, 0)
            pe.wait_ge(gate_loaded, 96)
            nc.tensor.transpose(out_bank[:, 0:CH + NE], bias_rows[:], ident[0:CH + NE, 0:CH + NE]
                                ).then_inc(bias_turned, 1)
            gate_logits(0)
            turn_comb(0)
            pe.wait_ge(bias_saved, 1)
            up(0, 0, True)
            up(0, 1, True)

            def body(i, start, end):
                for c in range(2 * CH):
                    p, k = c // CH, c % CH
                    g = 2 * i + p
                    if not (end and p == 1):
                        if k == 16:
                            turn_x(g + 1, 1 - p, i + p)
                        if k == 20:
                            gate_logits(g + 1)
                        if k == 30:
                            turn_comb(g + 1)
                    if k == 5 and not (start and p == 0):
                        turn_out(g - 1, 1 - p)
                    if not end or c + 2 < 2 * CH:
                        up(i, c + 2, start)
                    down(i, c, start)

            loop(pe, body)
            turn_out(NG - 1, 1)


_INS = ["attn_x", "attn_q1_w", "attn_q2_w", "attn_k1_w", "attn_k2_w", "attn_v_w", "attn_c_w",
        "attn_lambda_q1", "attn_lambda_k1", "attn_lambda_q2", "attn_lambda_k2",
        "ffn_gate_w", "ffn_gate_b", "ffn_w1", "ffn_b1", "ffn_w2", "ffn_b2",
        "ffn_ws1", "ffn_bs1", "ffn_ws2", "ffn_bs2"]


def kernel(**inputs):
    import numpy as np
    import concourse.bacc as bacc
    from concourse.bass_utils import run_bass_kernel_spmd

    nc = bacc.Bacc("TRN2", target_bir_lowering=False, num_devices=1)
    arrays, args = {}, []
    for name in _INS:
        a = np.ascontiguousarray(inputs["L0_" + name])
        arrays[f"in_{name}"] = a
        args.append(nc.dram_tensor(f"in_{name}", a.shape, mybir.dt.from_np(a.dtype), kind="ExternalInput").ap())
    args.append(nc.dram_tensor("out", (B, T, C), F32, kind="ExternalOutput").ap())
    build(nc, *args)
    r = run_bass_kernel_spmd(nc, [arrays], core_ids=[0])
    return r.results[0]["out"]
```
